# Optimizing a Trainium2 kernel written in Bass

```python
import numpy as np
import jax
import jax.numpy as jnp

def _softmax(x, axis=-1):
    return jax.nn.softmax(x, axis=axis)

def _gelu(x):
    return jax.nn.gelu(x, approximate=True)

def _silu(x):
    return jax.nn.silu(x)

def _sigmoid(x):
    return jax.nn.sigmoid(x)

def _layernorm(x, axis=-1, eps=1e-05):
    m = jnp.mean(x, axis=axis, keepdims=True)
    v = jnp.var(x, axis=axis, keepdims=True)
    return (x - m) / jnp.sqrt(v + eps)

def _scatter_add(tgt, idx, src, axis=0):
    return tgt.at[idx].add(src)

def _segment_sum(src, seg, n):
    return jax.ops.segment_sum(src, seg, n)
kernel_name = 'mk_early_fusion_d1_tok_img1024_r4_fcc297'

def setup_inputs(seed: int=0):
    np.random.seed(seed)
    _w = jnp.asarray

    def _rec_inputs():
        import jax
        import jax.numpy as jnp
        _rk = jax.random.key(seed)
        x = -0.00016672 + 0.999947 * jax.random.normal(jax.random.fold_in(_rk, 1), (32, 96, 96, 3), jnp.float32)
        txt = -3.39011e-05 + 0.925824 * jax.random.normal(jax.random.fold_in(_rk, 2), (32, 77, 256), jnp.float32)
        return (x, txt)
    x, txt = _rec_inputs()

    def _L0_tok_setup():
        import jax, jax.numpy as jnp
        import numpy as np
        B, H, W_IMG, C = (64, 96, 96, 3)
        P1, P2 = (16, 16)
        DIM_OUT = 256
        DIM_PATCH = P1 * P2 * C

        def patchify(x, p1, p2):
            bb, s1, s2, d = x.shape
            n1, n2 = (s1 // p1, s2 // p2)
            x = x.reshape(bb, n1, p1, n2, p2, d)
            x = x.transpose(0, 1, 3, 2, 4, 5)
            return (x.reshape(bb, n1 * n2, p1 * p2 * d), [n1, n2])
        key = jax.random.key(seed)
        k1, k2 = jax.random.split(key)
        x = jax.random.normal(k1, (B, H, W_IMG, C), dtype=jnp.float32)
        limit = float(np.sqrt(6.0 / (DIM_PATCH + DIM_OUT)))
        W = jax.random.uniform(k2, (DIM_OUT, DIM_PATCH), dtype=jnp.float32, minval=-limit, maxval=limit)
        b = jnp.zeros((DIM_OUT,), dtype=jnp.float32)
        return {'x': x, 'W': W, 'b': b}
    _L0_tok_all = _L0_tok_setup()
    _L0_tok_in = {k: v for k, v in _L0_tok_all.items() if k in ('W', 'b')}
    del _L0_tok_all

    def _L0_attn_setup():
        import jax, jax.numpy as jnp
        import numpy as np
        B, T, C, NH = (32, 128, 256, 16)
        DH = C // NH

        def _rope_tables(seq_len, dim):
            inv = 1.0 / 10000.0 ** (np.arange(0, dim, 2, dtype=np.float32) / dim)
            freqs = np.arange(seq_len, dtype=np.float32)[:, None] * inv[None, :]
            return (jnp.asarray(np.cos(freqs)), jnp.asarray(np.sin(freqs)))

        def _apply_rope(x, cos, sin):
            b, t, h, d = x.shape
            d2 = d // 2
            xv = x.reshape(b, t, h, d2, 2)
            x0, x1 = (xv[..., 0], xv[..., 1])
            c = cos[None, :t, None, :]
            s = sin[None, :t, None, :]
            o0 = x0 * c - x1 * s
            o1 = x0 * s + x1 * c
            return jnp.stack([o0, o1], axis=-1).reshape(b, t, h, d)
        key = jax.random.key(seed)
        ks = jax.random.split(key, 5)
        scale = 0.02
        return {'x': jax.random.normal(ks[0], (B, T, C), dtype=jnp.float32), 'Wq': jax.random.normal(ks[1], (C, C), dtype=jnp.float32) * scale, 'Wk': jax.random.normal(ks[2], (C, C), dtype=jnp.float32) * scale, 'Wv': jax.random.normal(ks[3], (C, C), dtype=jnp.float32) * scale, 'Wo': jax.random.normal(ks[4], (C, C), dtype=jnp.float32) * scale}
    _L0_attn_all = _L0_attn_setup()
    _L0_attn_in = {k: v for k, v in _L0_attn_all.items() if k in ('Wq', 'Wk', 'Wv', 'Wo')}
    del _L0_attn_all

    def _L0_ffn_setup():
        import jax, jax.numpy as jnp
        import numpy as np
        T, Z, D_DIM = (8, 512, 256)
        N_EXP, P_SLOT, H = (64, 32, 256)
        LN_EPS = 1e-05
        key = jax.random.key(seed)
        k = jax.random.split(key, 5)
        s = 0.02
        return {'x': jax.random.normal(k[0], (T, Z, D_DIM), dtype=jnp.float32), 'phi_w': jax.random.normal(k[1], (N_EXP * P_SLOT, D_DIM), dtype=jnp.float32) * s, 'phi_b': jax.random.normal(k[2], (N_EXP * P_SLOT,), dtype=jnp.float32) * s, 'expert_w': jax.random.normal(k[3], (N_EXP, D_DIM, H), dtype=jnp.float32) * s, 'expert_b': jax.random.normal(k[4], (N_EXP, H), dtype=jnp.float32) * s}
    _L0_ffn_all = _L0_ffn_setup()
    _L0_ffn_in = {k: v for k, v in _L0_ffn_all.items() if k in ('phi_w', 'phi_b', 'expert_w', 'expert_b')}
    del _L0_ffn_all
    return {'x': x, 'txt': txt, 'L0_tok_W': _L0_tok_in['W'], 'L0_tok_b': _L0_tok_in['b'], 'L0_attn_Wq': _L0_attn_in['Wq'], 'L0_attn_Wk': _L0_attn_in['Wk'], 'L0_attn_Wv': _L0_attn_in['Wv'], 'L0_attn_Wo': _L0_attn_in['Wo'], 'L0_ffn_phi_w': _L0_ffn_in['phi_w'], 'L0_ffn_phi_b': _L0_ffn_in['phi_b'], 'L0_ffn_expert_w': _L0_ffn_in['expert_w'], 'L0_ffn_expert_b': _L0_ffn_in['expert_b']}

def reference(x, txt, L0_tok_W, L0_tok_b, L0_attn_Wq, L0_attn_Wk, L0_attn_Wv, L0_attn_Wo, L0_ffn_phi_w, L0_ffn_phi_b, L0_ffn_expert_w, L0_ffn_expert_b):
    import jax
    import jax.numpy as jnp

    def _L0_tok_ref(x, W, b):
        import jax, jax.numpy as jnp
        import numpy as np
        B, H, W_IMG, C = (64, 96, 96, 3)
        P1, P2 = (16, 16)
        DIM_OUT = 256
        DIM_PATCH = P1 * P2 * C

        def patchify(x, p1, p2):
            bb, s1, s2, d = x.shape
            n1, n2 = (s1 // p1, s2 // p2)
            x = x.reshape(bb, n1, p1, n2, p2, d)
            x = x.transpose(0, 1, 3, 2, 4, 5)
            return (x.reshape(bb, n1 * n2, p1 * p2 * d), [n1, n2])
        patches, n_list = patchify(x, P1, P2)
        out = jnp.einsum('bnk,ok->bno', patches, W) + b
        return out

    def _L0_attn_ref(x, Wq, Wk, Wv, Wo):
        import jax, jax.numpy as jnp
        import numpy as np
        B, T, C, NH = (32, 128, 256, 16)
        DH = C // NH

        def _rope_tables(seq_len, dim):
            inv = 1.0 / 10000.0 ** (np.arange(0, dim, 2, dtype=np.float32) / dim)
            freqs = np.arange(seq_len, dtype=np.float32)[:, None] * inv[None, :]
            return (jnp.asarray(np.cos(freqs)), jnp.asarray(np.sin(freqs)))

        def _apply_rope(x, cos, sin):
            b, t, h, d = x.shape
            d2 = d // 2
            xv = x.reshape(b, t, h, d2, 2)
            x0, x1 = (xv[..., 0], xv[..., 1])
            c = cos[None, :t, None, :]
            s = sin[None, :t, None, :]
            o0 = x0 * c - x1 * s
            o1 = x0 * s + x1 * c
            return jnp.stack([o0, o1], axis=-1).reshape(b, t, h, d)
        b, t, c = x.shape
        cos, sin = _rope_tables(t, DH)
        q = (x @ Wq.T).reshape(b, t, NH, DH)
        k = (x @ Wk.T).reshape(b, t, NH, DH)
        v = (x @ Wv.T).reshape(b, t, NH, DH)
        q = _apply_rope(q, cos, sin)
        k = _apply_rope(k, cos, sin)
        q = q.transpose(0, 2, 1, 3)
        k = k.transpose(0, 2, 1, 3)
        v = v.transpose(0, 2, 1, 3)
        att = jnp.einsum('bhqd,bhkd->bhqk', q.astype(jnp.float32), k.astype(jnp.float32))
        att = att * DH ** (-0.5)
        att = jax.nn.softmax(att, axis=-1).astype(v.dtype)
        out = jnp.einsum('bhqk,bhkd->bhqd', att, v)
        out = out.transpose(0, 2, 1, 3).reshape(b, t, c)
        return out @ Wo.T

    def _L0_ffn_ref(x, phi_w, phi_b, expert_w, expert_b):
        import jax, jax.numpy as jnp
        import numpy as np
        T, Z, D_DIM = (8, 512, 256)
        N_EXP, P_SLOT, H = (64, 32, 256)
        LN_EPS = 1e-05
        t, z, d = x.shape
        n = expert_w.shape[0]
        p = phi_w.shape[0] // n
        logits = (jnp.einsum('tzd,ed->tze', x, phi_w) + phi_b).reshape(t, z, n, p)
        D = jax.nn.softmax(logits, axis=3)
        C = jax.nn.softmax(logits, axis=2)
        X_tilde = jnp.einsum('tznp,tzd->npd', D, x)
        X_tilde = jnp.clip(X_tilde, -33000.0, 65000.0)
        mu = jnp.mean(X_tilde, axis=-1, keepdims=True)
        var = jnp.mean(jnp.square(X_tilde - mu), axis=-1, keepdims=True)
        X_tilde = (X_tilde - mu) * jax.lax.rsqrt(var + LN_EPS)
        X_tilde = jnp.tanh(X_tilde)
        Y_tilde = jnp.einsum('npd,ndH->npH', X_tilde, expert_w) + expert_b[:, None, :]
        Y = jnp.einsum('tznp,npH->tzH', C, Y_tilde)
        return Y
    h = _L0_tok_ref(x, L0_tok_W, L0_tok_b)
    h = jnp.concatenate([h, txt], axis=1)
    h = h + _L0_attn_ref(_layernorm(h, axis=-1), L0_attn_Wq, L0_attn_Wk, L0_attn_Wv, L0_attn_Wo)
    h = h + _L0_ffn_ref(_layernorm(h, axis=-1), L0_ffn_phi_w, L0_ffn_phi_b, L0_ffn_expert_w, L0_ffn_expert_b)
    return h

_drawn_inputs = setup_inputs


def setup_inputs(seed=0):
    import zlib

    import numpy as np

    out = dict(_drawn_inputs(seed))
    spreads = {'L0_tok_b': (0.0, 0.1)}
    factors = {'L0_attn_Wq': 8.0, 'L0_attn_Wk': 8.0, 'L0_ffn_phi_b': 31.073}
    for name, (base, spread) in spreads.items():
        noise = np.random.default_rng([zlib.crc32(name.encode()), seed]).standard_normal(out[name].shape)
        drawn = base * np.exp(spread * noise) if base else spread * noise
        out[name] = jnp.asarray(drawn.astype(out[name].dtype))
    for name, factor in factors.items():
        out[name] = (out[name] * factor).astype(out[name].dtype)
    return out
```

```python
import numpy as np
import concourse.bass as bass
from concourse import mybir
from contextlib import ExitStack

F32 = mybir.dt.float32
F32R = mybir.dt.float32r
ALU = mybir.AluOpType
ACT = mybir.ActivationFunctionType
AX_X = mybir.AxisListType.X

BATCH, PATCHES, WORDS, C = 32, 36, 77, 256
T = PATCHES + WORDS
TOKENS = BATCH * T
PDIM = 16 * 16 * 3
KP = PDIM // 128
KC = C // 128
HEADS, DH = 16, 16
EXPERTS, SLOTS = 64, 32
E = EXPERTS * SLOTS
EB = E // 128
EPB = 128 // SLOTS
EPS = 1e-5
CLIP_LO, CLIP_HI = -33000.0, 65000.0
GH = 4
GROUPS = HEADS // GH
TE = T + 1
FULL_TILES = TOKENS // 128
TAIL = TOKENS - FULL_TILES * 128
TILES = FULL_TILES + 1
TG = 4


class Count:

    def __init__(self, k, per, rest):
        self.k, self.per, self.rest = k, per, rest

    def __add__(self, n):
        return Count(self.k, self.per, self.rest + n)

    __radd__ = __add__

    def __sub__(self, n):
        return self + -n

    def __mul__(self, n):
        return Count(self.k, self.per * n, self.rest * n)

    __rmul__ = __mul__


def val(n):
    return n if isinstance(n, int) else n.k * n.per + n.rest


def head_of(g, j):
    return 8 * (g // 2) + 2 * j + g % 2


def embed(nc, patches, wt, bias_row, emb, loads):
    tiles = BATCH * PATCHES // 128
    with ExitStack() as ctx:
        sb = lambda name, shape, dt=F32: ctx.enter_context(nc.sbuf_tensor(f"embed_{name}", shape, dt))
        sem = lambda name: ctx.enter_context(nc.semaphore(f"embed_{name}"))
        px = sb("px", [128, 2, KP, 128])
        wt_sb = sb("wt_sb", [128, KP, C])
        bias = sb("tok_bias", [128, C])
        emb_sb = sb("emb_sb", [128, 2, C])
        raw = [sb(f"raw{n}", list(hi.shape)) for n, (_, hi, _) in enumerate(loads)]
        acc = [ctx.enter_context(nc.psum_tensor(f"embed_acc{i}", [128, C], F32)) for i in range(2)]
        px_in = [sem("px_in0"), sem("px_in1")]
        w_in, b_in = sem("tok_w_in"), sem("tok_b_in")
        raw_in = [sem(f"raw_in{n}") for n in range(len(loads))]
        hi_done, lo_done = sem("hi_done"), sem("lo_done")
        mm_done, emb_ready, emb_out = sem("emb_mm"), sem("emb_ready"), [sem("emb_out0"), sem("emb_out1")]
        block = ctx.enter_context(nc.Block())

        @block.sync
        def _(sp):
            sp.dma_start(wt_sb[:], wt).then_inc(w_in, 16)
            sp.dma_start(bias[:], bias_row.broadcast_to([128, C])).then_inc(b_in, 16)
            for t in range(tiles + 2):
                if t < tiles:
                    if t >= 2:
                        sp.wait_ge(mm_done, t - 1)
                    sp.dma_start(px[:, t % 2], patches[t]).then_inc(px_in[t % 2], 16)
                if t >= 2:
                    sp.wait_ge(emb_ready, t - 1)
                    sp.dma_start(emb[(t - 2) * 128:(t - 1) * 128, :], emb_sb[:, t % 2]).then_inc(emb_out[t % 2], 16)
            for i in range(2):
                sp.wait_ge(emb_out[i], 16 * ((tiles + 1 - i) // 2))

        @block.scalar
        def _(act):
            for n, (src, _, _) in enumerate(loads):
                act.dma_start(raw[n][:], src).then_inc(raw_in[n], 16)
            for n, (_, hi, _) in enumerate(loads):
                act.wait_ge(raw_in[n], 16)
                nc.scalar.activation(hi[:], raw[n][:], ACT.Copy).then_inc(hi_done, 1)

        @block.gpsimd
        def _(pool):
            for n, (_, hi, lo) in enumerate(loads):
                pool.wait_ge(hi_done, val(n + 1))
                nc.gpsimd.tensor_tensor(lo[:], raw[n][:], hi[:].bitcast(F32), ALU.subtract).then_inc(lo_done, 1)
            pool.wait_ge(lo_done, len(loads))

        @block.tensor
        def _(pe):
            pe.wait_ge(w_in, 16)
            for t in range(tiles):
                pe.wait_ge(px_in[t % 2], val(16 * (t // 2 + 1)))
                if t >= 2:
                    pe.wait_ge(emb_ready, val(t - 1))
                for k in range(KP):
                    last = nc.tensor.matmul(acc[t % 2][:], px[:, t % 2, k, :], wt_sb[:, k, :],
                                            start=k == 0, stop=k == KP - 1)
                last.then_inc(mm_done, 1)

        @block.vector
        def _(dve):
            dve.wait_ge(b_in, 16)
            for t in range(tiles):
                dve.wait_ge(mm_done, val(t + 1))
                if t >= 2:
                    dve.wait_ge(emb_out[t % 2], val(16 * (t // 2)))
                nc.vector.tensor_tensor(emb_sb[:, t % 2], acc[t % 2][:], bias[:], ALU.add).then_inc(emb_ready, 1)


def attend(nc, emb, txt, rope_cos, rope_sin, ident, wqk, wv, wo, h2):
    (wqk_hi, wqk_lo), (wv_hi, wv_lo), (wo_hi, wo_lo) = wqk, wv, wo
    with ExitStack() as ctx:
        sb = lambda name, shape, dt=F32: ctx.enter_context(nc.sbuf_tensor(f"attend_{name}", shape, dt))
        pb = lambda name, shape: ctx.enter_context(nc.psum_tensor(f"attend_{name}", shape, F32))
        sem = lambda name: ctx.enter_context(nc.semaphore(f"attend_{name}"))
        h_in = [sb(f"h_in{i}", [T, C]) for i in range(2)]
        h_res = [sb(f"h_res{i}", [T, C]) for i in range(2)]
        h_out = [sb(f"h_out{i}", [T, C]) for i in range(2)]
        cos = sb("cos", [T, DH])
        sin = sb("sin", [T, DH])
        stats, mv, rstd = sb("stats", [T, 6]), sb("mv", [T, 2]), sb("rstd", [T, 1])
        power, eps = sb("power", [T, 1]), sb("eps", [T, 1])
        xn = [sb(f"xn{i}", [T, C]) for i in range(2)]
        xt_hi = [sb(f"xt_hi{i}", [128, KC, T], F32R) for i in range(2)]
        xt_lo = [sb(f"xt_lo{i}", [128, KC, T], F32R) for i in range(2)]
        rope_a, rope_b = sb("rope_a", [T, 2 * HEADS, DH]), sb("rope_b", [T, 2 * HEADS, DH])
        turned = sb("turned", [T, 2 * HEADS, DH])
        stack = [sb(f"stack{i}", [T, 2, HEADS, 64]) for i in range(2)]
        qt = [sb(f"qt{i}", [128, HEADS // 2, TE], F32R) for i in range(2)]
        kt = [sb(f"kt{i}", [128, HEADS // 2, TE], F32R) for i in range(2)]
        vp = [sb(f"vp{i}", [T, HEADS, 32]) for i in range(2)]
        smax = sb("smax", [T, 2, GH])
        prob = [sb(f"prob{i}", [T, GH, T]) for i in range(2)]
        prob_t = [sb(f"prob_t{i}", [T, GH, T]) for i in range(2)]
        ot_sb = sb("ot_sb", [128, GROUPS, T])
        rz = sb("rz", [T, GROUPS, GH])
        on = sb("on", [T, GROUPS, GH, DH])
        ont_hi = sb("ont_hi", [128, KC, T], F32R)
        ont_lo = sb("ont_lo", [128, KC, T], F32R)

        p_score = [pb(f"p_score{i}", [T, GH, TE]) for i in range(2)]
        p_turn = [pb(f"p_turn{i}", [128, 4, T]) for i in range(2)]
        p_qk = pb("p_qk", [T, 2 * HEADS * DH])
        p_v = pb("p_v", [T, 2, C])
        p_ot = pb("p_ot", [128, GROUPS, T])
        p_misc = pb("p_misc", [128, 512])
        xt_ps = p_misc[:, 0:KC * T].rearrange("p (k t) -> p k t", k=KC)

        tables_in = sem("tables_in")
        h_ld = [sem("h_ld0"), sem("h_ld1")]
        hr_ld = [sem("hr_ld0"), sem("hr_ld1")]
        h2_out = [sem("h2_out0"), sem("h2_out1")]
        consts = sem("consts")
        stats_ok, mv_ok, xn_ok = sem("stats_ok"), sem("mv_ok"), sem("xn_ok")
        var_ok, rstd_ok = sem("var_ok"), sem("rstd_ok")
        xt_ps_ok, xt_hi_ok, xt_lo_ok = sem("xt_ps_ok"), sem("xt_hi_ok"), sem("xt_lo_ok")
        qk_ok, rope_ok, turned_ok, hi_ok, lo_ok = sem("qk_ok"), sem("rope_ok"), sem("turned_ok"), sem("hi_ok"), sem("lo_ok")
        qkt_ps_ok, qkt_ok = sem("qkt_ps_ok"), sem("qkt_ok")
        v_ps_ok, v_ok = sem("v_ps_ok"), sem("v_ok")
        score_ok, max_ok, sub_ok, exp_ok = sem("score_ok"), sem("max_ok"), sem("sub_ok"), sem("exp_ok")
        pt_ps_ok, pt_ok, pv_ok, ot_ok = sem("pt_ps_ok"), sem("pt_ok"), sem("pv_ok"), sem("ot_ok")
        o_ps_ok, rz_ok, on_ok = sem("o_ps_ok"), sem("rz_ok"), sem("on_ok")
        ont_ps_ok, ont_hi_ok, ont_lo_ok = sem("ont_ps_ok"), sem("ont_hi_ok"), sem("ont_lo_ok")
        wo_ok, h2_ok = sem("wo_ok"), sem("h2_ok")
        block = ctx.enter_context(nc.Block())

        def steps(eng, step):
            straight = lambda b: step(b, lambda n: (b + n) // 2, b % 2, b + 2 < BATCH, b + 1 < BATCH and b >= -1,
                                      0 <= b < BATCH, b >= 1)
            for b in range(-2, 3):
                straight(b)
            with eng.Fori(0, (BATCH - 6) // 2) as k:
                for c in (3, 4):
                    step(Count(k, 2, c), lambda n, c=c: Count(k, 1, (c + n) // 2), c % 2, True, True, True, True)
            for b in range(BATCH - 3, BATCH + 1):
                straight(b)

        @block.sync
        def _(sp):
            sp.dma_start(cos[:], rope_cos).then_inc(tables_in, 16)
            sp.dma_start(sin[:], rope_sin).then_inc(tables_in, 16)

            def load(dst, ld, b, par):
                sp.dma_start(dst[par][0:PATCHES, :], emb[bass.ds(val(b * PATCHES), PATCHES), :]).then_inc(ld[par], 16)
                sp.dma_start(dst[par][PATCHES:T, :], txt[bass.ds(val(b * WORDS), WORDS), :]).then_inc(ld[par], 16)

            for b in range(2):
                load(h_in, h_ld, b, b)

            def step(b, half, par, projects, turns, scores, finishes):
                if projects:
                    sp.wait_ge(xn_ok, val(b + 3))
                    if not isinstance(b, int) or b + 4 < BATCH:
                        load(h_in, h_ld, b + 4, par)
                if scores:
                    if not isinstance(b, int) or b >= 2:
                        sp.wait_ge(h2_ok, val(b - 1))
                    load(h_res, hr_ld, b, par)
                if finishes:
                    sp.wait_ge(h2_ok, val(b))
                    sp.dma_start(h2[bass.ds(val((b - 1) * T), T), :], h_out[1 - par][:]).then_inc(h2_out[1 - par], 16)

            for b in (-2, -1, 0, 1):
                step(b, None, b % 2, True, True, b >= 0, b >= 1)
            with sp.Fori(0, (BATCH - 6) // 2) as k:
                for c in (2, 3):
                    step(Count(k, 2, c), None, c % 2, True, True, True, True)
            for b in range(BATCH - 4, BATCH + 1):
                step(b, None, b % 2, b + 2 < BATCH, True, b < BATCH, True)
            for i in range(2):
                sp.wait_ge(h2_out[i], 16 * (BATCH // 2))

        @block.vector
        def _(dve):
            dve.wait_ge(tables_in, 32)
            for i in range(2):
                nc.vector.memset(stack[i][:], 0.0)
                nc.vector.memset(qt[i][:].bitcast(F32), 0.0)
                nc.vector.memset(kt[i][:].bitcast(F32), 0.0)
                nc.vector.memset(vp[i][:], 0.0).then_inc(consts, 1)
            dve.wait_ge(consts, 2)
            for i in range(2):
                nc.vector.memset(vp[i][:, :, DH:DH + 1], 1.0)
            nc.vector.memset(eps[:], EPS)
            nc.vector.memset(power[:], -0.5).then_inc(consts, 1)

            def softmax_in(b, g):
                dve.wait_ge(score_ok, val(GROUPS * b + g + 1))
                nc.vector.reduce_max(smax[:, g % 2], p_score[g % 2][:, :, 0:T], AX_X).then_inc(max_ok, 1)
                dve.wait_ge(max_ok, val(GROUPS * b + g + 1))
                if g >= 2:
                    dve.wait_ge(pt_ps_ok, val(GROUPS * b + g - 1))
                elif not isinstance(b, int) or b >= 1:
                    dve.wait_ge(pt_ps_ok, val(GROUPS * b + g - 1))
                nc.vector.tensor_tensor(prob[g % 2][:], p_score[g % 2][:, :, 0:T],
                                        smax[:, g % 2].unsqueeze(2).broadcast_to([T, GH, T]),
                                        ALU.subtract).then_inc(sub_ok, 1)

            def step(b, half, par, projects, turns, scores, finishes):
                if projects:
                    dve.wait_ge(h_ld[par], val(32 * (half(2) + 1)))
                    nc.vector.bn_stats(stats[:], h_in[par][:]).then_inc(stats_ok, 1)
                    dve.drain()
                    nc.vector.bn_aggr(mv[:], stats[:]).then_inc(mv_ok, 1)
                if scores:
                    softmax_in(b, 0)
                if projects:
                    dve.wait_ge(rstd_ok, val(b + 3))
                    if not isinstance(b, int) or b >= 0:
                        dve.wait_ge(xt_ps_ok, val(b + 1))
                    nc.vector.tensor_scalar(xn[par][:], h_in[par][:], mv[:, 0:1], rstd[:], ALU.subtract,
                                            ALU.mult).then_inc(xn_ok, 1)
                if scores:
                    softmax_in(b, 1)
                if projects:
                    dve.wait_ge(xt_hi_ok, val(b + 3))
                    if not isinstance(b, int) or b >= 0:
                        dve.wait_ge(v_ps_ok, val(b + 1))
                    nc.vector.tensor_tensor(xt_lo[par][:], xt_ps, xt_hi[par][:].bitcast(F32),
                                            ALU.subtract).then_inc(xt_lo_ok, 1)
                if scores:
                    softmax_in(b, 2)
                if projects:
                    dve.wait_ge(qk_ok, val(b + 3))
                    if not isinstance(b, int) or b >= -1:
                        dve.wait_ge(turned_ok, val(b + 2))
                    qk3 = p_qk[:].rearrange("p (h d) -> p h d", d=DH)
                    nc.vector.tensor_tensor(rope_a[:], qk3, cos[:].unsqueeze(1).broadcast_to([T, 2 * HEADS, DH]),
                                            ALU.mult)
                    for e in range(2):
                        last = nc.vector.tensor_tensor(
                            rope_b[:].rearrange("p h (i e) -> p h i e", e=2)[:, :, :, e],
                            qk3.rearrange("p h (i e) -> p h i e", e=2)[:, :, :, 1 - e],
                            sin[:].rearrange("p (i e) -> p i e", e=2)[:, :, e].unsqueeze(1).broadcast_to(
                                [T, 2 * HEADS, DH // 2]), ALU.mult)
                    last.then_inc(rope_ok, 1)
                if scores:
                    softmax_in(b, 3)
                if finishes:
                    o_ps = p_misc[0:T, :].rearrange("p (g j d) -> p g j d", g=GROUPS, j=GH)
                    dve.wait_ge(o_ps_ok, val(b))
                    nc.vector.reciprocal(rz[:], o_ps[:, :, :, DH]).then_inc(rz_ok, 1)
                    dve.wait_ge(rz_ok, val(b))
                    if not isinstance(b, int) or b >= 2:
                        dve.wait_ge(ont_ps_ok, val(b - 1))
                    nc.vector.tensor_tensor(on[:], o_ps[:, :, :, 0:DH],
                                            rz[:].unsqueeze(3).broadcast_to([T, GROUPS, GH, DH]),
                                            ALU.mult).then_inc(on_ok, 1)
                    dve.wait_ge(ont_hi_ok, val(b))
                    if not isinstance(b, int) or b >= 2:
                        dve.wait_ge(wo_ok, val(b - 1))
                    nc.vector.tensor_tensor(ont_lo[:], xt_ps, ont_hi[:].bitcast(F32), ALU.subtract).then_inc(ont_lo_ok, 1)
                    dve.wait_ge(wo_ok, val(b))
                    dve.wait_ge(hr_ld[1 - par], val(32 * (half(-1) + 1)))
                    if not isinstance(b, int) or b >= 3:
                        dve.wait_ge(h2_out[1 - par], val(16 * half(-1)))
                    nc.vector.tensor_tensor(h_out[1 - par][:], p_v[:, 1, :], h_res[1 - par][:], ALU.add).then_inc(h2_ok, 1)

            steps(dve, step)

        @block.gpsimd
        def _(pool):
            pool.wait_ge(consts, 3)

            def step(b, half, par, projects, turns, scores, finishes):
                if projects:
                    pool.wait_ge(mv_ok, val(b + 3))
                    nc.gpsimd.tensor_tensor(mv[:, 1:2], mv[:, 1:2], eps[:], ALU.add).then_inc(var_ok, 1)
                    pool.wait_ge(var_ok, val(b + 3))
                    if not isinstance(b, int) or b >= -1:
                        pool.wait_ge(xn_ok, val(b + 2))
                    nc.gpsimd.tensor_tensor(rstd[:], mv[:, 1:2], power[:], ALU.pow).then_inc(rstd_ok, 1)
                    pool.wait_ge(rope_ok, val(b + 3))
                    if not isinstance(b, int) or b >= -1:
                        pool.wait_ge(hi_ok, val(2 * (b + 2)))
                    nc.gpsimd.tensor_tensor(turned[:], rope_a[:], rope_b[:], ALU.add).then_inc(turned_ok, 1)
                    for s, slot in ((0, 2), (1, 1)):
                        pool.wait_ge(hi_ok, val(2 * (b + 2) + s + 1))
                        nc.gpsimd.tensor_tensor(stack[par][:, s, :, slot * DH:(slot + 1) * DH].bitcast(F32R),
                                                turned[:, s * HEADS:(s + 1) * HEADS, :],
                                                stack[par][:, s, :, 0:DH], ALU.subtract).then_inc(lo_ok, 1)

            steps(pool, step)
            pool.wait_ge(lo_ok, 2 * BATCH)

        @block.scalar
        def _(act):
            act.wait_ge(consts, 3)

            def exp_group(b, g):
                act.wait_ge(sub_ok, val(GROUPS * b + g + 1))
                nc.scalar.activation(prob[g % 2][:], prob[g % 2][:], ACT.Exp, scale=DH ** -0.5).then_inc(exp_ok, 1)

            def keep_prob_t(b, g):
                act.wait_ge(pt_ps_ok, val(GROUPS * b + g + 1))
                if g >= 2 or not isinstance(b, int) or b >= 1:
                    act.wait_ge(pv_ok, val(GROUPS * b + g - 1))
                nc.scalar.activation(prob_t[g % 2][:], p_turn[g % 2][0:T], ACT.Copy).then_inc(pt_ok, 1)

            def keep_qkt(b, par, n):
                act.wait_ge(qkt_ps_ok, val(4 * (b + 1) + n + 1))
                if n == 0 and (not isinstance(b, int) or b >= 1):
                    act.wait_ge(score_ok, val(GROUPS * b))
                dst = (qt if n < 2 else kt)[1 - par]
                nc.scalar.activation(dst[:, 4 * (n % 2):4 * (n % 2) + 4, 0:T], p_turn[n % 2][:], ACT.Copy).then_inc(qkt_ok, 1)

            def step(b, half, par, projects, turns, scores, finishes):
                if scores:
                    exp_group(b, 0)
                    exp_group(b, 1)
                if projects:
                    act.wait_ge(xt_ps_ok, val(b + 3))
                    if not isinstance(b, int) or b >= 0:
                        act.wait_ge(v_ps_ok, val(b + 1))
                    nc.scalar.activation(xt_hi[par][:], xt_ps, ACT.Copy).then_inc(xt_hi_ok, 1)
                if scores:
                    keep_prob_t(b, 0)
                    keep_prob_t(b, 1)
                if turns:
                    keep_qkt(b, par, 0)
                    keep_qkt(b, par, 1)
                if scores:
                    exp_group(b, 2)
                    keep_prob_t(b, 2)
                if scores:
                    exp_group(b, 3)
                    keep_prob_t(b, 3)
                if turns:
                    keep_qkt(b, par, 2)
                    keep_qkt(b, par, 3)
                    act.wait_ge(v_ps_ok, val(b + 2))
                    if not isinstance(b, int) or b >= 1:
                        act.wait_ge(pv_ok, val(GROUPS * b))
                    nc.scalar.activation(vp[1 - par][:, :, 0:DH], p_v[:, 0, :].rearrange("p (h d) -> p h d", d=DH),
                                         ACT.Copy).then_inc(v_ok, 1)
                if projects:
                    act.wait_ge(turned_ok, val(b + 3))
                    if not isinstance(b, int) or b >= 0:
                        act.wait_ge(qkt_ps_ok, val(4 * (b + 1)))
                    for s, step_ in ((0, 1), (1, 2)):
                        dst = stack[par][:, s].rearrange("p h (r d) -> p h r d", d=DH)[:, :, 0:step_ + 1:step_, :]
                        src = turned[:, s * HEADS:(s + 1) * HEADS, :].unsqueeze(2).broadcast_to([T, HEADS, 2, DH])
                        nc.scalar.activation(dst.bitcast(F32R), src, ACT.Copy).then_inc(hi_ok, 1)
                if finishes:
                    act.wait_ge(ont_ps_ok, val(b))
                    if not isinstance(b, int) or b >= 2:
                        act.wait_ge(wo_ok, val(b - 1))
                    nc.scalar.activation(ont_hi[:], xt_ps, ACT.Copy).then_inc(ont_hi_ok, 1)
                if scores:
                    act.wait_ge(pv_ok, val(GROUPS * (b + 1)))
                    if not isinstance(b, int) or b >= 1:
                        act.wait_ge(o_ps_ok, val(b))
                    nc.scalar.activation(ot_sb[:], p_ot[:], ACT.Copy).then_inc(ot_ok, 1)

            steps(act, step)

        @block.tensor
        def _(pe):
            pe.wait_ge(consts, 3)

            def score(b, par, g):
                if g >= 2 or not isinstance(b, int) or b >= 1:
                    pe.wait_ge(sub_ok, val(GROUPS * b + g - 1))
                base = 64 * (g % 2)
                for j in range(GH):
                    h = head_of(g, j)
                    last = nc.tensor.matmul(p_score[g % 2][:, j, :], qt[par][base:base + 3 * DH, h // 2, 0:T],
                                            kt[par][base:base + 3 * DH, h // 2, :], start=True, stop=True)
                last.then_inc(score_ok, 1)

            def turn_probs(b, g):
                pe.wait_ge(exp_ok, val(GROUPS * b + g + 1))
                for j in range(GH):
                    last = nc.tensor.transpose(p_turn[g % 2][0:T, j, :], prob[g % 2][:, j, :], ident[0:T, 0:T])
                last.then_inc(pt_ps_ok, 1)

            def weigh_values(b, par, g):
                pe.wait_ge(pt_ok, val(GROUPS * b + g + 1))
                for j in range(GH):
                    last = nc.tensor.matmul(p_ot[32 * j:32 * j + 32, g, :], vp[par][:, head_of(g, j), :],
                                            prob_t[g % 2][:, j, :], start=True, stop=True)
                last.then_inc(pv_ok, 1)

            def turn_qk(b, par, n):
                for i in range(4):
                    hp = 4 * (n % 2) + i
                    last = nc.tensor.transpose(p_turn[n % 2][:, i, :],
                                               stack[1 - par][:, n // 2, 2 * hp:2 * hp + 2, :], ident[0:T, 0:T])
                last.then_inc(qkt_ps_ok, 1)

            def split_product(out, hi, lo, w_hi, w_lo):
                n = 0
                for a, w in ((hi, w_hi), (hi, w_lo), (lo, w_hi)):
                    for k in range(KC):
                        last = nc.tensor.matmul(out, a[:, k, :], w[:, k, :], start=n == 0, stop=n == 3 * KC - 1)
                        n += 1
                return last

            def step(b, half, par, projects, turns, scores, finishes):
                first = isinstance(b, int)
                if scores:
                    pe.wait_ge(qkt_ok, val(4 * (b + 1)))
                    score(b, par, 0)
                    score(b, par, 1)
                if projects:
                    pe.wait_ge(xn_ok, val(b + 3))
                    if not first or b >= -1:
                        pe.wait_ge(xt_lo_ok, val(b + 2))
                    if not first or b >= 2:
                        pe.wait_ge(ont_lo_ok, val(b - 1))
                    for k in range(KC):
                        last = nc.tensor.transpose(xt_ps[:, k, :], xn[par][:, 128 * k:128 * k + 128], ident[0:T, 0:T])
                    last.then_inc(xt_ps_ok, 1)
                if scores:
                    pe.wait_ge(qkt_ok, val(4 * b + 4))
                    turn_probs(b, 0)
                    turn_probs(b, 1)
                    score(b, par, 2)
                    score(b, par, 3)
                if projects:
                    pe.wait_ge(xt_lo_ok, val(b + 3))
                    if not first or b >= -1:
                        pe.wait_ge(rope_ok, val(b + 2))
                    split_product(p_qk[:], xt_hi[par], xt_lo[par], wqk_hi, wqk_lo).then_inc(qk_ok, 1)
                if turns:
                    pe.wait_ge(lo_ok, val(2 * (b + 2)))
                    if scores:
                        pe.wait_ge(pt_ok, val(GROUPS * b + 2))
                    turn_qk(b, par, 0)
                    turn_qk(b, par, 1)
                if scores:
                    if not first or b >= 1:
                        pe.wait_ge(ot_ok, val(b))
                    pe.wait_ge(v_ok, val(b + 1))
                    weigh_values(b, par, 0)
                    weigh_values(b, par, 1)
                    if turns:
                        pe.wait_ge(qkt_ok, val(4 * (b + 1) + 2))
                    turn_probs(b, 2)
                    turn_probs(b, 3)
                    weigh_values(b, par, 2)
                    weigh_values(b, par, 3)
                if turns:
                    if scores:
                        pe.wait_ge(pt_ok, val(GROUPS * (b + 1)))
                    else:
                        pe.wait_ge(qkt_ok, val(4 * (b + 1) + 2))
                    turn_qk(b, par, 2)
                    turn_qk(b, par, 3)
                    if not first or b >= 2:
                        pe.wait_ge(h2_ok, val(b - 1))
                    if not first or b >= 0:
                        pe.wait_ge(v_ok, val(b + 1))
                    split_product(p_v[:, 0, :], xt_hi[1 - par], xt_lo[1 - par], wv_hi, wv_lo).then_inc(v_ps_ok, 1)
                if finishes:
                    pe.wait_ge(ot_ok, val(b))
                    if projects:
                        pe.wait_ge(xt_lo_ok, val(b + 3))
                    for g in range(GROUPS):
                        last = nc.tensor.transpose(p_misc[0:T, 128 * g:128 * g + 128], ot_sb[:, g, :], ident[:, :])
                    last.then_inc(o_ps_ok, 1)
                    pe.wait_ge(on_ok, val(b))
                    for k in range(KC):
                        last = nc.tensor.transpose(xt_ps[:, k, :], on[:].rearrange("p g j d -> p (g j d)")[:, 128 * k:128 * k + 128],
                                                   ident[0:T, 0:T])
                    last.then_inc(ont_ps_ok, 1)
                    pe.wait_ge(ont_lo_ok, val(b))
                    if turns:
                        pe.wait_ge(v_ok, val(b + 2))
                    split_product(p_v[:, 1, :], ont_hi, ont_lo, wo_hi, wo_lo).then_inc(wo_ok, 1)

            steps(pe, step)


def dispatch(nc, h2, phi, slot_bias, ident, xacc, ct_out):
    phi_hi, phi_lo = phi
    bias_rows, bias_ones = slot_bias
    with ExitStack() as ctx:
        sb = lambda name, shape, dt=F32: ctx.enter_context(nc.sbuf_tensor(f"dispatch_{name}", shape, dt))
        pb = lambda name, shape: ctx.enter_context(nc.psum_tensor(f"dispatch_{name}", shape, F32))
        sem = lambda name: ctx.enter_context(nc.semaphore(f"dispatch_{name}"))
        RING = 2 * TG
        h_t = [sb(f"h_t{i}", [128, C]) for i in range(2)]
        xn = [sb(f"xn{i}", [128, C]) for i in range(2)]
        x = [sb(f"x{i}", [128, C]) for i in range(RING)]
        stats, mv, rstd, power = sb("stats", [128, 6]), sb("mv", [128, 2]), sb("rstd", [128, 1]), sb("power", [128, 1])
        eps = sb("eps", [128, 1])
        xt_hi, xt_lo = sb("xt_hi", [128, KC, 128], F32R), sb("xt_lo", [128, KC, 128], F32R)
        dmax, cmax = sb("dmax", [128, EXPERTS]), sb("cmax", [128, SLOTS])
        dsum, csum = sb("dsum", [128, 2, EXPERTS]), sb("csum", [128, 2, SLOTS])
        disp = [sb(f"disp{i}", [128, EXPERTS, SLOTS]) for i in range(RING)]
        comb = [sb(f"comb{i}", [128, EXPERTS, SLOTS]) for i in range(2)]
        ct = [sb(f"ct{i}", [128, EB, 128]) for i in range(2)]

        logits = pb("logits", [128, EXPERTS, SLOTS])
        p_turn = [pb(f"p_turn{i}", [128, 4, 128]) for i in range(2)]
        p_sum = [pb(f"p_sum{i}", [128, 2, C]) for i in range(2)]
        NB = 4
        XB = EXPERTS // NB
        bank = lambda c: slice(c * XB, (c + 1) * XB)

        consts = sem("consts")
        h_ld, ct_st = [sem("h_ld0"), sem("h_ld1")], [sem("ct_st0"), sem("ct_st1")]
        stats_ok, mv_ok, var_ok, rstd_ok, x_ok = sem("stats_ok"), sem("mv_ok"), sem("var_ok"), sem("rstd_ok"), sem("x_ok")
        xt_ps_ok, xt_hi_ok, xt_lo_ok = sem("xt_ps_ok"), sem("xt_hi_ok"), sem("xt_lo_ok")
        logit_ok, dmax_ok, dsub_ok, cmax_ok, csub_ok = sem("logit_ok"), sem("dmax_ok"), sem("dsub_ok"), sem("cmax_ok"), sem("csub_ok")
        dexp_ok, cexp_ok, dsum_ok, csum_ok = sem("dexp_ok"), sem("cexp_ok"), sem("dsum_ok"), sem("csum_ok")
        drec_ok, crec_ok, disp_ok, comb_ok = sem("drec_ok"), sem("crec_ok"), sem("disp_ok"), sem("comb_ok")
        kept_ok = sem("kept_ok")
        ct_ps_ok, ct_ok, sum_ok, acc_ok = sem("ct_ps_ok"), sem("ct_ok"), sem("sum_ok"), sem("acc_ok")
        block = ctx.enter_context(nc.Block())
        UNITS = EB // 2
        PER = UNITS // TG

        def steps(eng, step):
            straight = lambda t: step(t, lambda n: (t + n) // 2, t, TAIL if t == FULL_TILES else 128)
            for t in range(-1, TG):
                straight(t)
            with eng.Fori(0, (FULL_TILES - TG) // RING) as k:
                for c in range(TG, TG + RING):
                    step(Count(k, RING, c), lambda n, c=c: Count(k, TG, (c + n) // 2), c, 128)
            straight(FULL_TILES)
            straight(FULL_TILES + 1)

        static = lambda t: isinstance(t, int)

        def products_of(n, xc):
            return PER * (n - xc % TG) - UNITS

        def sums(t, c):
            if not static(t):
                return [(2 * t - UNITS + i, PER * (c % TG) + i) for i in range(PER)]
            if t < TG:
                return []
            g = FULL_TILES // TG - 1 + t - FULL_TILES
            return [(UNITS * g + u, u) for u in range(UNITS)]

        @block.sync
        def _(sp):
            def load(t, par, rows=128):
                sp.dma_start(h_t[par][0:rows], h2[bass.ds(val(t * 128), rows), :]).then_inc(h_ld[par], 16)

            load(0, 0)
            load(1, 1)

            def store(t, par, rows):
                for q in range(4):
                    sp.wait_ge(ct_ok, val(4 * t + q + 1))
                    sp.dma_start(ct_out[bass.ds(val(t * 128), 128), 4 * q:4 * q + 4, 0:rows],
                                 ct[par][:, 4 * q:4 * q + 4, 0:rows]).then_inc(ct_st[par], 16)

            def step(t, half, c, rows):
                if not static(t) or t + 3 < TILES:
                    if static(t) and t < 0:
                        sp.wait_ge(x_ok, 1)
                        load(2, 0)
                    else:
                        sp.wait_ge(x_ok, val(t + 2))
                        load(t + 3, (c + 3) % 2, TAIL if static(t) and t + 3 == FULL_TILES else 128)
                if not static(t) or t >= 1:
                    store(t - 1, (c + 1) % 2,
                          TAIL if static(t) and t - 1 == FULL_TILES else 128)

            for t in range(-1, TG):
                step(t, None, t, 128)
            with sp.Fori(0, (FULL_TILES - 2 * TG) // TG) as k:
                for c in range(TG, 2 * TG):
                    step(Count(k, TG, c), None, c, 128)
            for t in range(FULL_TILES - TG, FULL_TILES + 2):
                step(t, None, t, 128)
            sp.wait_ge(ct_st[0], 64 * ((TILES + 1) // 2))
            sp.wait_ge(ct_st[1], 64 * (TILES // 2))

        @block.vector
        def _(dve):
            for i in range(2):
                nc.vector.memset(xacc[:, i * EB // 2:(i + 1) * EB // 2, :], 0.0).then_inc(acc_ok, 1)
            nc.vector.memset(eps[:], EPS)
            nc.vector.memset(power[:], -0.5).then_inc(consts, 1)
            dve.wait_ge(acc_ok, 2)

            def norm(n, par, xc, rows, half):
                dve.wait_ge(h_ld[par], val(16 * (half + 1)))
                nc.vector.bn_stats(stats[0:rows], h_t[par][0:rows]).then_inc(stats_ok, 1)
                dve.drain()
                nc.vector.bn_aggr(mv[0:rows], stats[0:rows]).then_inc(mv_ok, 1)

            def norm_end(n, par, xc, rows):
                dve.wait_ge(rstd_ok, val(n + 1))
                if not static(n) or n >= 2:
                    dve.wait_ge(kept_ok, val(n - 1))
                    dve.wait_ge(xt_ps_ok, val(n - 1))
                nc.vector.tensor_scalar(xn[xc % 2][0:rows], h_t[par][0:rows], mv[0:rows, 0:1], rstd[0:rows],
                                        ALU.subtract, ALU.mult).then_inc(x_ok, 1)

            def keep_sum(s, u):
                dve.wait_ge(sum_ok, val(s + 1))
                nc.vector.tensor_tensor(xacc[:, 2 * u:2 * u + 2, :], p_sum[u % 2][:], xacc[:, 2 * u:2 * u + 2, :],
                                        ALU.add).then_inc(acc_ok, 1)

            def step(t, half, c, rows):
                live = not static(t) or 0 <= t < TILES
                more = not static(t) or t + 1 < TILES
                nrows = TAIL if static(t) and t + 1 == FULL_TILES else 128
                if live:
                    for b in range(NB):
                        dve.wait_ge(logit_ok, val(NB * t + b + 1))
                        nc.vector.reduce_max(dmax[0:rows, bank(b)], logits[0:rows, bank(b), :], AX_X).then_inc(dmax_ok, 1)
                        dve.wait_ge(dmax_ok, val(NB * t + b + 1))
                        if b == 0 and (not static(t) or t >= RING):
                            dve.wait_ge(acc_ok, val(products_of(t, c) + 2))
                        nc.vector.tensor_tensor(disp[c % RING][0:rows, bank(b), :], logits[0:rows, bank(b), :],
                                                dmax[0:rows, bank(b)].unsqueeze(2).broadcast_to([rows, XB, SLOTS]),
                                                ALU.subtract).then_inc(dsub_ok, 1)
                    nc.vector.reduce_max(cmax[0:rows], logits[0:rows].rearrange("p n s -> p s n"), AX_X).then_inc(cmax_ok, 1)
                    dve.wait_ge(cmax_ok, val(t + 1))
                    if not static(t) or t >= 2:
                        dve.wait_ge(ct_ps_ok, val(4 * (t - 1)))
                    for b in range(NB):
                        nc.vector.tensor_tensor(comb[c % 2][0:rows, bank(b), :], logits[0:rows, bank(b), :],
                                                cmax[0:rows].unsqueeze(1).broadcast_to([rows, XB, SLOTS]),
                                                ALU.subtract).then_inc(csub_ok, 1)
                if more:
                    norm(t + 1, (c + 1) % 2, c + 1, nrows, half(1))
                if live:
                    dve.wait_ge(dexp_ok, val(2 * (t + 1)))
                    if not static(t) or t >= 1:
                        dve.wait_ge(disp_ok, val(t))
                    nc.vector.reduce_sum(dsum[0:rows, 0], disp[c % RING][0:rows], AX_X).then_inc(dsum_ok, 1)
                if more:
                    norm_end(t + 1, (c + 1) % 2, c + 1, nrows)
                if live:
                    dve.wait_ge(dsum_ok, val(t + 1))
                    nc.vector.reciprocal(dsum[0:rows, 1], dsum[0:rows, 0]).then_inc(drec_ok, 1)
                    dve.wait_ge(cexp_ok, val(2 * (t + 1)))
                    if not static(t) or t >= 1:
                        dve.wait_ge(comb_ok, val(t))
                    nc.vector.reduce_sum(csum[0:rows, 0], comb[c % 2][0:rows].rearrange("p n s -> p s n"), AX_X).then_inc(csum_ok, 1)
                    dve.wait_ge(csum_ok, val(t + 1))
                    nc.vector.reciprocal(csum[0:rows, 1], csum[0:rows, 0]).then_inc(crec_ok, 1)
                if more:
                    dve.wait_ge(xt_hi_ok, val(t + 2))
                    nc.vector.tensor_tensor(xt_lo[:, :, 0:nrows], p_turn[0][:, 0:KC, 0:nrows],
                                            xt_hi[:, :, 0:nrows].bitcast(F32), ALU.subtract).then_inc(xt_lo_ok, 1)
                for s, u in sums(t, c):
                    keep_sum(s, u)

            steps(dve, step)

        @block.gpsimd
        def _(pool):
            pool.wait_ge(consts, 1)

            def step(t, half, c, rows):
                live = not static(t) or 0 <= t < TILES
                more = not static(t) or t + 1 < TILES
                nrows = TAIL if static(t) and t + 1 == FULL_TILES else 128
                if more:
                    pool.wait_ge(mv_ok, val(t + 2))
                    nc.gpsimd.tensor_tensor(mv[0:nrows, 1:2], mv[0:nrows, 1:2], eps[0:nrows], ALU.add).then_inc(var_ok, 1)
                    pool.wait_ge(var_ok, val(t + 2))
                    nc.gpsimd.tensor_tensor(rstd[0:nrows], mv[0:nrows, 1:2], power[0:nrows], ALU.pow).then_inc(rstd_ok, 1)
                if live:
                    pool.wait_ge(drec_ok, val(t + 1))
                    d = disp[c % RING][0:rows]
                    nc.gpsimd.tensor_tensor(d, d, dsum[0:rows, 1].unsqueeze(2).broadcast_to([rows, EXPERTS, SLOTS]),
                                            ALU.mult).then_inc(disp_ok, 1)
                    pool.wait_ge(crec_ok, val(t + 1))
                    m = comb[c % 2][0:rows]
                    nc.gpsimd.tensor_tensor(m, m, csum[0:rows, 1].unsqueeze(1).broadcast_to([rows, EXPERTS, SLOTS]),
                                            ALU.mult).then_inc(comb_ok, 1)

            steps(pool, step)

        @block.scalar
        def _(act):
            def step(t, half, c, rows):
                live = not static(t) or 0 <= t < TILES
                more = not static(t) or t + 1 < TILES
                nrows = TAIL if static(t) and t + 1 == FULL_TILES else 128
                two = lambda i: slice(2 * i * XB, 2 * (i + 1) * XB)
                if live:
                    for i in range(2):
                        act.wait_ge(dsub_ok, val(NB * t + 2 * i + 2))
                        d = disp[c % RING][0:rows, two(i), :]
                        nc.scalar.activation(d, d, ACT.Exp).then_inc(dexp_ok, 1)
                    for i in range(2):
                        act.wait_ge(csub_ok, val(NB * t + 2 * i + 2))
                        m = comb[c % 2][0:rows, two(i), :]
                        nc.scalar.activation(m, m, ACT.Exp).then_inc(cexp_ok, 1)
                if not static(t) or t >= 1:
                    prow = TAIL if static(t) and t - 1 == FULL_TILES else 128
                    for q in range(4):
                        act.wait_ge(ct_ps_ok, val(4 * (t - 1) + q + 1))
                        if q == 0 and (not static(t) or t >= 3):
                            act.wait_ge(ct_st[(c + 1) % 2], val(64 * half(-1)))
                        nc.scalar.activation(ct[(c + 1) % 2][:, 4 * q:4 * q + 4, 0:prow], p_turn[q % 2][:, :, 0:prow],
                                             ACT.Copy).then_inc(ct_ok, 1)
                if more:
                    act.wait_ge(xt_ps_ok, val(t + 2))
                    if not static(t) or t >= 0:
                        act.wait_ge(logit_ok, val(NB * (t + 1)))
                    nc.scalar.activation(xt_hi[:, :, 0:nrows], p_turn[0][:, 0:KC, 0:nrows], ACT.Copy).then_inc(xt_hi_ok, 1)
                if live:
                    act.wait_ge(x_ok, val(t + 1))
                    if not static(t) or t >= RING:
                        act.wait_ge(acc_ok, val(products_of(t, c) + 2))
                    nc.scalar.activation(x[c % RING][0:rows], xn[c % 2][0:rows], ACT.Copy).then_inc(kept_ok, 1)

            steps(act, step)

        @block.tensor
        def _(pe):
            def step(t, half, c, rows):
                live = not static(t) or 0 <= t < TILES
                more = not static(t) or t + 1 < TILES
                nrows = TAIL if static(t) and t + 1 == FULL_TILES else 128
                if live:
                    pe.wait_ge(xt_lo_ok, val(t + 1))
                    for b in range(NB):
                        if not static(t) or t >= 1:
                            pe.wait_ge(csub_ok, val(NB * (t - 1) + b + 1))
                        out = logits[0:rows, bank(b), :]
                        cols = slice(512 * b, 512 * (b + 1))
                        nc.tensor.matmul(out, bias_ones[:, 0:rows], bias_rows[:, cols], start=True, stop=False)
                        for i, (a, w) in enumerate(((xt_hi, phi_hi), (xt_hi, phi_lo), (xt_lo, phi_hi))):
                            for k in range(KC):
                                last = nc.tensor.matmul(out, a[:, k, 0:rows], w[:, k, cols], start=False,
                                                        stop=i == 2 and k == KC - 1)
                        last.then_inc(logit_ok, 1)
                if not static(t) or t >= 1:
                    prow = TAIL if static(t) and t - 1 == FULL_TILES else 128
                    pe.wait_ge(comb_ok, val(t))
                    flat = comb[(c + 1) % 2][0:prow].rearrange("p n s -> p (n s)")
                    for q in range(4):
                        if q >= 2:
                            pe.wait_ge(ct_ok, val(4 * (t - 1) + q - 1))
                        elif q == 0 and (not static(t) or t < TILES):
                            pe.wait_ge(xt_lo_ok, val(t + 1))
                        elif q == 0:
                            pe.wait_ge(ct_ok, val(4 * (t - 1)))
                        if q == 1 and (not static(t) or t >= 2):
                            pe.wait_ge(ct_ok, val(4 * (t - 1)))
                        for i in range(4):
                            e = 4 * q + i
                            last = nc.tensor.transpose(p_turn[q % 2][:, i, 0:prow], flat[:, 128 * e:128 * e + 128],
                                                       ident[0:prow, 0:prow])
                        last.then_inc(ct_ps_ok, 1)
                if more:
                    pe.wait_ge(x_ok, val(t + 2))
                    if not static(t) or t >= 1:
                        pe.wait_ge(ct_ok, val(4 * (t - 1) + 3))
                    for k in range(KC):
                        last = nc.tensor.transpose(p_turn[0][:, k, 0:nrows], xn[(c + 1) % 2][0:nrows, 128 * k:128 * k + 128],
                                                   ident[0:nrows, 0:nrows])
                    last.then_inc(xt_ps_ok, 1)
                tail = static(t) and t == FULL_TILES + 1
                for m, (s, u) in enumerate(sums(t, c)):
                    if tail:
                        tiles, n = [FULL_TILES % RING], TAIL
                    else:
                        g = (c // TG + 1) % 2
                        tiles, n = range(TG * g, TG * g + TG), 128
                    if m == 0:
                        pe.wait_ge(disp_ok, val(FULL_TILES + 1 if tail else t - c % TG))
                        pe.wait_ge(kept_ok, val(FULL_TILES + 1 if tail else t - c % TG))
                    pe.wait_ge(acc_ok, val(s + 1))
                    for i in range(2):
                        e = 2 * u + i
                        for n_th, d in enumerate(tiles):
                            last = nc.tensor.matmul(p_sum[u % 2][:, i, :],
                                                    disp[d][0:n].rearrange("p n s -> p (n s)")[:, 128 * e:128 * e + 128],
                                                    x[d][0:n], start=n_th == 0, stop=n_th == len(tiles) - 1)
                    last.then_inc(sum_ok, 1)

            steps(pe, step)


def experts(nc, xacc, wexp, ebias, ident, y_hi, y_lo):
    with ExitStack() as ctx:
        sb = lambda name, shape, dt=F32: ctx.enter_context(nc.sbuf_tensor(f"experts_{name}", shape, dt))
        pb = lambda name, shape: ctx.enter_context(nc.psum_tensor(f"experts_{name}", shape, F32))
        sem = lambda name: ctx.enter_context(nc.semaphore(f"experts_{name}"))
        RING = 8
        w = [sb(f"w{i}", [128, EPB, KC, C]) for i in range(RING)]
        eb = sb("eb", [128, EB, C])
        stats, mv, rstd = sb("stats", [128, EB, 6]), sb("mv", [128, EB, 2]), sb("rstd", [128, EB])
        power = sb("power", [128, EB])
        xs = sb("xs", [128, EB, C])
        xst = [sb(f"xst{i}", [128, KC, 128]) for i in range(2)]
        y = sb("y", [128, 2, C])
        p_t = [pb(f"p_t{i}", [128, KC, 128]) for i in range(2)]
        p_y = [pb(f"p_y{i}", [128, C]) for i in range(2)]
        eb_in, w_in = sem("eb_in"), [sem(f"w_in{i}") for i in range(RING)]
        clip_ok, stats_ok, mv_ok, var_ok, rstd_ok = sem("clip_ok"), sem("stats_ok"), sem("mv_ok"), sem("var_ok"), sem("rstd_ok")
        consts, norm_ok, tanh_ok, t_ps_ok, t_ok = sem("consts"), sem("norm_ok"), sem("tanh_ok"), sem("t_ps_ok"), sem("t_ok")
        y_ps_ok, y_ok, hi_ok, lo_ok = sem("y_ps_ok"), sem("y_ok"), sem("hi_ok"), sem("lo_ok")
        block = ctx.enter_context(nc.Block())

        @block.sync
        def _(sp):
            for j in range(EPB):
                sp.dma_start(eb[SLOTS * j:SLOTS * (j + 1)], ebias[j:j + 1].broadcast_to([SLOTS, EB, C])).then_inc(eb_in, 16)
            for i in range(EB):
                if i >= RING:
                    sp.wait_ge(y_ps_ok, i - RING + 1)
                sp.dma_start(w[i % RING][:], wexp[i]).then_inc(w_in[i % RING], 16)

        @block.vector
        def _(dve):
            nc.vector.memset(power[:], -0.5).then_inc(consts, 1)
            nc.vector.tensor_scalar(xacc[:], xacc[:], CLIP_LO, CLIP_HI, ALU.max, ALU.min).then_inc(clip_ok, 1)
            dve.wait_ge(clip_ok, 1)
            for i in range(EB):
                nc.vector.bn_stats(stats[:, i], xacc[:, i]).then_inc(stats_ok, 1)
            dve.wait_ge(stats_ok, EB)
            for i in range(EB):
                nc.vector.bn_aggr(mv[:, i], stats[:, i]).then_inc(mv_ok, 1)
            dve.wait_ge(rstd_ok, 1)
            for i in range(EB):
                nc.vector.tensor_scalar(xs[:, i], xacc[:, i], mv[:, i, 0:1], rstd[:, i:i + 1], ALU.subtract,
                                        ALU.mult).then_inc(norm_ok, 1)
            dve.wait_ge(eb_in, 16 * EPB)
            for i in range(EB):
                dve.wait_ge(y_ps_ok, i + 1)
                if i >= 2:
                    dve.wait_ge(lo_ok, i - 1)
                nc.vector.tensor_tensor(y[:, i % 2], p_y[i % 2][:], eb[:, i], ALU.add).then_inc(y_ok, 1)

        @block.gpsimd
        def _(pool):
            pool.wait_ge(consts, 1)
            pool.wait_ge(mv_ok, EB)
            nc.gpsimd.tensor_scalar(mv[:, :, 1], mv[:, :, 1], EPS, None, ALU.add).then_inc(var_ok, 1)
            pool.wait_ge(var_ok, 1)
            nc.gpsimd.tensor_tensor(rstd[:], mv[:, :, 1], power[:], ALU.pow).then_inc(rstd_ok, 1)
            for i in range(EB):
                pool.wait_ge(hi_ok, i + 1)
                nc.gpsimd.tensor_tensor(y_lo[:, i], y[:, i % 2], y_hi[:, i].bitcast(F32), ALU.subtract).then_inc(lo_ok, 1)
            pool.wait_ge(lo_ok, EB)

        @block.scalar
        def _(act):
            for i in range(EB):
                act.wait_ge(norm_ok, i + 1)
                nc.scalar.activation(xs[:, i], xs[:, i], ACT.Tanh).then_inc(tanh_ok, 1)
            for i in range(EB + 1):
                if i < EB:
                    act.wait_ge(t_ps_ok, i + 1)
                    if i >= 2:
                        act.wait_ge(y_ps_ok, i - 1)
                    nc.scalar.activation(xst[i % 2][:], p_t[i % 2][:], ACT.Copy).then_inc(t_ok, 1)
                if i >= 1:
                    act.wait_ge(y_ok, i)
                    nc.scalar.activation(y_hi[:, i - 1], y[:, (i - 1) % 2], ACT.Copy).then_inc(hi_ok, 1)

        @block.tensor
        def _(pe):
            for i in range(EB + 1):
                if i < EB:
                    pe.wait_ge(tanh_ok, i + 1)
                    if i >= 2:
                        pe.wait_ge(t_ok, i - 1)
                    for k in range(KC):
                        last = nc.tensor.transpose(p_t[i % 2][:, k], xs[:, i, 128 * k:128 * k + 128], ident[:, :])
                    last.then_inc(t_ps_ok, 1)
                if i >= 1:
                    n = i - 1
                    pe.wait_ge(t_ok, val(n + 1))
                    pe.wait_ge(w_in[n % RING], val(16 * (n // RING + 1)))
                    if n >= 2:
                        pe.wait_ge(y_ok, val(n - 1))
                    for k in range(KC):
                        for j in range(EPB):
                            last = nc.tensor.matmul(p_y[n % 2][SLOTS * j:SLOTS * (j + 1), :],
                                                    xst[n % 2][:, k, SLOTS * j:SLOTS * (j + 1)],
                                                    w[n % RING][:, j, k, :], start=k == 0, stop=k == KC - 1)
                    last.then_inc(y_ps_ok, 1)


def combine(nc, ct_in, h2, y_hi, y_lo, out):
    with ExitStack() as ctx:
        sb = lambda name, shape, dt=F32: ctx.enter_context(nc.sbuf_tensor(f"combine_{name}", shape, dt))
        sem = lambda name: ctx.enter_context(nc.semaphore(f"combine_{name}"))
        RING = 4
        raw = [sb(f"raw{i}", [128, EB, 128]) for i in range(RING)]
        h_t = [sb(f"h_t{i}", [128, C]) for i in range(RING)]
        hi = [sb(f"hi{i}", [128, EB, 128], F32R) for i in range(2)]
        lo = [sb(f"lo{i}", [128, EB, 128], F32R) for i in range(2)]
        o = [sb(f"o{i}", [128, C]) for i in range(2)]
        p_o = [ctx.enter_context(nc.psum_tensor(f"combine_p_o{i}", [128, C], F32)) for i in range(2)]
        ld, h_ld, st = [sem(f"ld{i}") for i in range(RING)], [sem(f"h_ld{i}") for i in range(RING)], [sem("st0"), sem("st1")]
        hi_ok, lo_ok, mm_ok, o_ok = sem("hi_ok"), sem("lo_ok"), sem("mm_ok"), sem("o_ok")
        block = ctx.enter_context(nc.Block())
        static = lambda t: isinstance(t, int)

        def steps(eng, step):
            for t in range(RING):
                step(t, 0, t, 128)
            with eng.Fori(0, FULL_TILES // RING - 1) as k:
                for c in range(RING):
                    step(Count(k, RING, RING + c), Count(k, 1, 1), c, 128)
            step(FULL_TILES, FULL_TILES // RING, 0, TAIL)

        @block.sync
        def _(sp):
            def step(t, turn, c, rows):
                if not static(t) or t >= RING:
                    sp.wait_ge(lo_ok, val(t - RING + 1))
                sp.dma_start(raw[c][:, :, 0:rows], ct_in[bass.ds(val(t * 128), 128), :, 0:rows]).then_inc(ld[c], 16)
                if not static(t) or t >= RING:
                    sp.wait_ge(o_ok, val(t - RING + 1))
                sp.dma_start(h_t[c][0:rows], h2[bass.ds(val(t * 128), rows), :]).then_inc(h_ld[c], 16)

            steps(sp, step)

        @block.scalar
        def _(act):
            def step(t, turn, c, rows):
                act.wait_ge(ld[c], val(16 * (turn + 1)))
                if not static(t) or t >= 2:
                    act.wait_ge(mm_ok, val(t - 1))
                nc.scalar.activation(hi[c % 2][:, :, 0:rows], raw[c][:, :, 0:rows], ACT.Copy).then_inc(hi_ok, 1)

            steps(act, step)

        @block.vector
        def _(dve):
            def finish(t, turn, c, rows):
                dve.wait_ge(mm_ok, val(t + 1))
                dve.wait_ge(h_ld[c], val(16 * (turn + 1)))
                if not static(t) or t >= 2:
                    dve.wait_ge(st[c % 2], val(16 * (2 * turn + c // 2)))
                nc.vector.tensor_tensor(o[c % 2][0:rows], p_o[c % 2][0:rows], h_t[c][0:rows], ALU.add).then_inc(o_ok, 1)

            def step(t, turn, c, rows):
                dve.wait_ge(hi_ok, val(t + 1))
                if not static(t) or t >= 2:
                    dve.wait_ge(mm_ok, val(t - 1))
                nc.vector.tensor_tensor(lo[c % 2][:, :, 0:rows], raw[c][:, :, 0:rows], hi[c % 2][:, :, 0:rows].bitcast(F32),
                                        ALU.subtract).then_inc(lo_ok, 1)
                if not static(t) or t >= 1:
                    finish(t - 1, turn if c else turn - 1, (c - 1) % RING, 128)

            steps(dve, step)
            finish(FULL_TILES, FULL_TILES // RING, 0, TAIL)

        @block.gpsimd
        def _(pool):
            def step(t, turn, c, rows):
                pool.wait_ge(o_ok, val(t + 1))
                pool.dma_start(out[bass.ds(val(t * 128), rows), :], o[c % 2][0:rows]).then_inc(st[c % 2], 16)

            steps(pool, step)
            pool.wait_ge(st[0], 16 * ((TILES + 1) // 2))
            pool.wait_ge(st[1], 16 * (TILES // 2))

        @block.tensor
        def _(pe):
            def step(t, turn, c, rows):
                pe.wait_ge(lo_ok, val(t + 1))
                if not static(t) or t >= 2:
                    pe.wait_ge(o_ok, val(t - 1))
                n = 0
                for a, y in ((hi, y_hi), (hi, y_lo), (lo, y_hi)):
                    for e in range(EB):
                        last = nc.tensor.matmul(p_o[c % 2][0:rows], a[c % 2][:, e, 0:rows], y[:, e, :],
                                                start=n == 0, stop=n == 3 * EB - 1)
                        n += 1
                last.then_inc(mm_ok, 1)

            steps(pe, step)


def program(nc, patches, txt, wt, tok_b, wqk, wv, wo, phi, phi_b, wexp, ebias, rope_cos, rope_sin, identity, out):
    emb = nc.dram_tensor("emb", (BATCH * PATCHES, C), F32, kind="Internal").ap()
    h2 = nc.dram_tensor("h2", (TOKENS, C), F32, kind="Internal").ap()
    ct = nc.dram_tensor("combine_t", (TILES * 128, EB, 128), F32, kind="Internal").ap()

    def parts(ctx, name, shape):
        return [ctx.enter_context(nc.sbuf_tensor(f"{name}_{part}", shape, F32R)) for part in ("hi", "lo")]

    with nc.sbuf_tensor("ident", [128, 128], F32) as ident, nc.sbuf_tensor("xacc", [128, EB, C], F32) as xacc:
        with ExitStack() as slots:
            phi_parts = parts(slots, "phi", [128, KC, E])
            bias_rows = slots.enter_context(nc.sbuf_tensor("bias_rows", [64, E], F32R))
            bias_ones = slots.enter_context(nc.sbuf_tensor("bias_ones", [64, 128], F32R))
            load_constants(nc, identity, ident, phi_b, bias_rows, bias_ones)
            with ExitStack() as projections:
                wqk_parts = parts(projections, "wqk", [128, KC, 2 * C])
                wv_parts = parts(projections, "wv", [128, KC, C])
                wo_parts = parts(projections, "wo", [128, KC, C])
                embed(nc, patches, wt, tok_b, emb, [(wqk, *wqk_parts), (wv, *wv_parts), (wo, *wo_parts),
                                                    (phi, *phi_parts)])
                attend(nc, emb, txt, rope_cos, rope_sin, ident, wqk_parts, wv_parts, wo_parts, h2)
            dispatch(nc, h2, phi_parts, (bias_rows, bias_ones), ident, xacc, ct)
        with ExitStack() as outputs:
            y_parts = parts(outputs, "y", [128, EB, C])
            experts(nc, xacc, wexp, ebias, ident, *y_parts)
            combine(nc, ct, h2, *y_parts, out)


def load_constants(nc, identity, ident, phi_b, bias_rows, bias_ones):
    with (nc.sbuf_tensor("bias_raw", [64, E], F32) as raw, nc.semaphore("in_ok") as in_ok,
          nc.semaphore("hi_ok") as hi_ok, nc.semaphore("zero_ok") as zero_ok, nc.semaphore("lo_ok") as lo_ok,
          nc.sbuf_tensor("bias_hi", [64, E], F32R) as hi, nc.Block() as block):

        @block.sync
        def _(sp):
            sp.dma_start(ident[:], identity).then_inc(in_ok, 16)
            sp.dma_start(raw[:], phi_b.broadcast_to([64, E])).then_inc(in_ok, 16)

        @block.vector
        def _(dve):
            nc.vector.memset(bias_rows[:].bitcast(F32), 0.0)
            nc.vector.memset(bias_ones[:].bitcast(F32), 1.0).then_inc(zero_ok, 1)
            dve.wait_ge(in_ok, 32)
            nc.vector.tensor_copy(hi[:], raw[:]).then_inc(hi_ok, 1)
            dve.wait_ge(hi_ok, 1)
            dve.wait_ge(zero_ok, 1)
            nc.vector.tensor_copy(bias_rows[0:1], raw[0:1])
            nc.vector.tensor_tensor(bias_rows[32:33], raw[32:33], hi[32:33].bitcast(F32), ALU.subtract).then_inc(lo_ok, 1)
            dve.wait_ge(lo_ok, 1)


def kernel(x, txt, L0_tok_W, L0_tok_b, L0_attn_Wq, L0_attn_Wk, L0_attn_Wv, L0_attn_Wo, L0_ffn_phi_w, L0_ffn_phi_b,
           L0_ffn_expert_w, L0_ffn_expert_b):
    import concourse.bacc as bacc
    from concourse.bass_utils import run_bass_kernel_spmd

    a = np.ascontiguousarray
    x, txt = np.asarray(x), np.asarray(txt)
    patches = x.reshape(BATCH, 6, 16, 6, 16, 3).transpose(0, 1, 3, 2, 4, 5).reshape(-1, 128, KP, 128).transpose(0, 3, 2, 1)

    def lead(w, k):
        w = np.asarray(w)
        return w.reshape(w.shape[0], k, 128).transpose(2, 1, 0)

    order = [head_of(g, j) for g in range(GROUPS) for j in range(GH)]
    wo = np.asarray(L0_attn_Wo).reshape(C, HEADS, DH)[:, order, :].reshape(C, C)
    wexp = np.asarray(L0_ffn_expert_w).reshape(EB, EPB, KC, 128, C).transpose(0, 3, 1, 2, 4)
    ebias = np.asarray(L0_ffn_expert_b).reshape(EB, EPB, C).transpose(1, 0, 2)
    inv = 1.0 / 10000.0 ** (np.arange(0, DH, 2, dtype=np.float32) / DH)
    freqs = np.arange(T, dtype=np.float32)[:, None] * inv[None, :]
    cos = np.repeat(np.cos(freqs), 2, axis=1).astype(np.float32)
    sin = np.stack([-np.sin(freqs), np.sin(freqs)], axis=-1).reshape(T, DH).astype(np.float32)
    arrays = {
        "patches": a(patches), "txt": a(txt.reshape(BATCH * WORDS, C)), "wt": a(lead(L0_tok_W, KP)),
        "tok_b": a(np.asarray(L0_tok_b).reshape(1, C)),
        "wqk": a(lead(np.concatenate([np.asarray(L0_attn_Wq), np.asarray(L0_attn_Wk)]), KC)),
        "wv": a(lead(L0_attn_Wv, KC)), "wo": a(lead(wo, KC)), "phi": a(lead(L0_ffn_phi_w, KC)),
        "phi_b": a(np.asarray(L0_ffn_phi_b).reshape(1, E)), "wexp": a(wexp), "ebias": a(ebias),
        "rope_cos": cos, "rope_sin": sin, "identity": np.eye(128, dtype=np.float32),
    }
    nc = bacc.Bacc("TRN2", target_bir_lowering=False, num_devices=1)
    args = {n: nc.dram_tensor(n, v.shape, mybir.dt.from_np(v.dtype), kind="ExternalInput").ap() for n, v in arrays.items()}
    out = nc.dram_tensor("out", (TOKENS, C), F32, kind="ExternalOutput").ap()
    program(nc, out=out, **args)
    r = run_bass_kernel_spmd(nc, [arrays], core_ids=[0])
    return r.results[0]["out"].reshape(BATCH, T, C)
```

```python
import numpy as np
import concourse.bass as bass
from concourse import mybir
from contextlib import ExitStack

F32 = mybir.dt.float32
F32R = mybir.dt.float32r
ALU = mybir.AluOpType
ACT = mybir.ActivationFunctionType
AX_X = mybir.AxisListType.X

BATCH, PATCHES, WORDS, C = 32, 36, 77, 256
T = PATCHES + WORDS
TOKENS = BATCH * T
PDIM = 16 * 16 * 3
KP = PDIM // 128
KC = C // 128
HEADS, DH = 16, 16
EXPERTS, SLOTS = 64, 32
E = EXPERTS * SLOTS
EB = E // 128
EPB = 128 // SLOTS
EPS = 1e-5
CLIP_LO, CLIP_HI = -33000.0, 65000.0
GH = 4
GROUPS = HEADS // GH
TE = T + 1
FULL_TILES = TOKENS // 128
TAIL = TOKENS - FULL_TILES * 128
TILES = FULL_TILES + 1
EXPERT_RING = 10
COMBINE_RING = 4
TG = 4


class Count:

    def __init__(self, k, per, rest):
        self.k, self.per, self.rest = k, per, rest

    def __add__(self, n):
        return Count(self.k, self.per, self.rest + n)

    __radd__ = __add__

    def __sub__(self, n):
        return self + -n

    def __mul__(self, n):
        return Count(self.k, self.per * n, self.rest * n)

    __rmul__ = __mul__


def val(n):
    return n if isinstance(n, int) else n.k * n.per + n.rest


def head_of(g, j):
    return 8 * (g // 2) + 2 * j + g % 2


def embed(nc, patches, wt, bias_row, emb, loads, identity, ident, slot_bias_row, bias_rows, bias_ones):
    tiles = BATCH * PATCHES // 128
    BANKS = 4
    with ExitStack() as ctx:
        sb = lambda name, shape, dt=F32: ctx.enter_context(nc.sbuf_tensor(f"embed_{name}", shape, dt))
        sem = lambda name: ctx.enter_context(nc.semaphore(f"embed_{name}"))
        px = sb("px", [128, tiles, KP, 128])
        wt_sb = sb("wt_sb", [128, KP, C])
        bias = sb("tok_bias", [128, C])
        emb_sb = sb("emb_sb", [128, tiles, C])
        raw = [sb(f"raw{n}", list(hi.shape)) for n, (_, hi, _) in enumerate(loads)]
        slot_raw, slot_hi = sb("slot_raw", [64, E]), sb("slot_hi", [64, E], F32R)
        acc = [ctx.enter_context(nc.psum_tensor(f"embed_acc{i}", [128, C], F32)) for i in range(BANKS)]
        px_in = [sem(f"px_in{t}") for t in range(tiles)]
        w_in, b_in = [sem("tok_w_in0"), sem("tok_w_in1")], sem("tok_b_in")
        ident_in, slot_in = sem("ident_in"), sem("slot_in")
        slot_zero_ok, slot_hi_ok, slot_ok = sem("slot_zero_ok"), sem("slot_hi_ok"), sem("slot_ok")
        raw_in = [sem(f"raw_in{n}") for n in range(len(loads))]
        hi_done, lo_done, half_done = sem("hi_done"), sem("lo_done"), sem("half_done")
        mm_done, emb_ready, emb_out = sem("emb_mm"), sem("emb_ready"), sem("emb_out")
        block = ctx.enter_context(nc.Block())

        @block.sync
        def _(sp):
            for i in range(2):
                part = slice(i * KP // 2, (i + 1) * KP // 2)
                sp.dma_start(wt_sb[:, part], wt[:, part]).then_inc(w_in[i], 16)
                if i == 0:
                    sp.dma_start(px[:, 0], patches[0]).then_inc(px_in[0], 16)
            sp.dma_start(bias[:], bias_row.broadcast_to([128, C])).then_inc(b_in, 16)
            for t in range(1, tiles):
                sp.dma_start(px[:, t], patches[t]).then_inc(px_in[t], 16)
            for t in range(tiles):
                sp.wait_ge(emb_ready, t + 1)
                sp.dma_start(emb[t * 128:(t + 1) * 128, :], emb_sb[:, t]).then_inc(emb_out, 16)
            sp.wait_ge(emb_out, 16 * tiles)
            sp.wait_ge(ident_in, 16)

        @block.scalar
        def _(act):
            act.wait_ge(px_in[tiles - 2], 16)
            act.dma_start(slot_raw[:], slot_bias_row.broadcast_to([64, E])).then_inc(slot_in, 16)
            act.dma_start(ident[:], identity).then_inc(ident_in, 16)
            for n, (src, _, _) in enumerate(loads):
                act.dma_start(raw[n][:], src).then_inc(raw_in[n], 16)
            for n, (_, hi, _) in enumerate(loads):
                act.wait_ge(raw_in[n], 16)
                nc.scalar.activation(hi[:], raw[n][:], ACT.Copy).then_inc(hi_done, 1)

        @block.gpsimd
        def _(pool):
            for n, (_, hi, lo) in enumerate(loads):
                pool.wait_ge(hi_done, n + 1)
                part = slice(0, KC // 2) if n == len(loads) - 1 else slice(0, KC)
                nc.gpsimd.tensor_tensor(lo[:, part], raw[n][:, part], hi[:, part].bitcast(F32),
                                        ALU.subtract).then_inc(lo_done, 1)
            pool.wait_ge(lo_done, len(loads))

        @block.tensor
        def _(pe):
            for t in range(tiles):
                pe.wait_ge(px_in[t], 16)
                if t >= BANKS:
                    pe.wait_ge(emb_ready, t - BANKS + 1)
                for k in range(KP):
                    if t == 0 and k % (KP // 2) == 0:
                        pe.wait_ge(w_in[k // (KP // 2)], 16)
                    last = nc.tensor.matmul(acc[t % BANKS][:], px[:, t, k, :], wt_sb[:, k, :],
                                            start=k == 0, stop=k == KP - 1)
                last.then_inc(mm_done, 1)

        @block.vector
        def _(dve):
            nc.vector.memset(bias_rows[:].bitcast(F32), 0.0)
            nc.vector.memset(bias_ones[:].bitcast(F32), 1.0).then_inc(slot_zero_ok, 1)
            dve.wait_ge(b_in, 16)
            for t in range(tiles):
                dve.wait_ge(mm_done, t + 1)
                nc.vector.tensor_tensor(emb_sb[:, t], acc[t % BANKS][:], bias[:], ALU.add).then_inc(emb_ready, 1)
                if t == tiles - 3:
                    dve.wait_ge(slot_in, 16)
                    nc.vector.tensor_copy(slot_hi[:], slot_raw[:]).then_inc(slot_hi_ok, 1)
                    dve.wait_ge(slot_hi_ok, 1)
                    dve.wait_ge(slot_zero_ok, 1)
                    nc.vector.tensor_copy(bias_rows[0:1], slot_raw[0:1]).then_inc(slot_ok, 1)
                    nc.vector.tensor_tensor(bias_rows[32:33], slot_raw[32:33], slot_hi[32:33].bitcast(F32),
                                            ALU.subtract).then_inc(slot_ok, 1)
            dve.wait_ge(slot_ok, 2)
            dve.wait_ge(hi_done, len(loads))
            _, hi, lo = loads[-1]
            nc.vector.tensor_tensor(lo[:, KC // 2:KC], raw[-1][:, KC // 2:KC], hi[:, KC // 2:KC].bitcast(F32),
                                    ALU.subtract).then_inc(half_done, 1)
            dve.wait_ge(half_done, 1)


def attend(nc, emb, txt, rope_cos, rope_sin, ident, wqk, wv, wo, h2):
    (wqk_hi, wqk_lo), (wv_hi, wv_lo), (wo_hi, wo_lo) = wqk, wv, wo
    with ExitStack() as ctx:
        sb = lambda name, shape, dt=F32: ctx.enter_context(nc.sbuf_tensor(f"attend_{name}", shape, dt))
        pb = lambda name, shape: ctx.enter_context(nc.psum_tensor(f"attend_{name}", shape, F32))
        sem = lambda name: ctx.enter_context(nc.semaphore(f"attend_{name}"))
        h_in = [sb(f"h_in{i}", [T, C]) for i in range(2)]
        h_res = [sb(f"h_res{i}", [T, C]) for i in range(2)]
        h_out = [sb(f"h_out{i}", [T, C]) for i in range(2)]
        cos = sb("cos", [T, DH])
        sin = sb("sin", [T, DH])
        stats, mv, rstd = sb("stats", [T, 6]), sb("mv", [T, 2]), sb("rstd", [T, 1])
        power, eps = sb("power", [T, 1]), sb("eps", [T, 1])
        xn = [sb(f"xn{i}", [T, C]) for i in range(2)]
        xt_hi = [sb(f"xt_hi{i}", [128, KC, T], F32R) for i in range(2)]
        xt_lo = [sb(f"xt_lo{i}", [128, KC, T], F32R) for i in range(2)]
        rope_a, rope_b = sb("rope_a", [T, 2 * HEADS, DH]), sb("rope_b", [T, 2 * HEADS, DH])
        turned = sb("turned", [T, 2 * HEADS, DH])
        stack = [sb(f"stack{i}", [T, 2, HEADS, 64]) for i in range(2)]
        qt = [sb(f"qt{i}", [128, HEADS // 2, TE], F32R) for i in range(2)]
        kt = [sb(f"kt{i}", [128, HEADS // 2, TE], F32R) for i in range(2)]
        vp = [sb(f"vp{i}", [T, HEADS, 32]) for i in range(2)]
        smax = sb("smax", [T, 2, GH])
        prob = [sb(f"prob{i}", [T, GH, T]) for i in range(2)]
        prob_t = [sb(f"prob_t{i}", [T, GH, T]) for i in range(2)]
        ot_sb = sb("ot_sb", [128, GROUPS, T])
        rz = sb("rz", [T, GROUPS, GH])
        on = sb("on", [T, GROUPS, GH, DH])
        ont_hi = sb("ont_hi", [128, KC, T], F32R)
        ont_lo = sb("ont_lo", [128, KC, T], F32R)

        p_score = [pb(f"p_score{i}", [T, GH, TE]) for i in range(2)]
        p_turn = [pb(f"p_turn{i}", [128, 4, T]) for i in range(2)]
        p_qk = pb("p_qk", [T, 2 * HEADS * DH])
        p_v = pb("p_v", [T, 2, C])
        p_ot = pb("p_ot", [128, GROUPS, T])
        p_misc = pb("p_misc", [128, 512])
        xt_ps = p_misc[:, 0:KC * T].rearrange("p (k t) -> p k t", k=KC)

        tables_in = sem("tables_in")
        h_ld = [sem("h_ld0"), sem("h_ld1")]
        hr_ld = [sem("hr_ld0"), sem("hr_ld1")]
        h2_out = [sem("h2_out0"), sem("h2_out1")]
        consts, values_clear, pads_ok, stack_clear, q_clear = sem("consts"), sem("values_clear"), sem("pads_ok"), sem("stack_clear"), sem("q_clear")
        stats_ok, mv_ok, xn_ok = sem("stats_ok"), sem("mv_ok"), sem("xn_ok")
        var_ok, rstd_ok = sem("var_ok"), sem("rstd_ok")
        xt_ps_ok, xt_hi_ok, xt_lo_ok = sem("xt_ps_ok"), sem("xt_hi_ok"), sem("xt_lo_ok")
        qk_ok, rope_ok, turned_ok, hi_ok, lo_ok = sem("qk_ok"), sem("rope_ok"), sem("turned_ok"), sem("hi_ok"), sem("lo_ok")
        qkt_ps_ok, qkt_ok = sem("qkt_ps_ok"), sem("qkt_ok")
        v_ps_ok, v_ok = sem("v_ps_ok"), sem("v_ok")
        score_ok, max_ok, sub_ok, exp_ok = sem("score_ok"), sem("max_ok"), sem("sub_ok"), sem("exp_ok")
        pt_ps_ok, pt_ok, pv_ok, ot_ok = sem("pt_ps_ok"), sem("pt_ok"), sem("pv_ok"), sem("ot_ok")
        o_ps_ok, rz_ok, on_ok = sem("o_ps_ok"), sem("rz_ok"), sem("on_ok")
        ont_ps_ok, ont_hi_ok, ont_lo_ok = sem("ont_ps_ok"), sem("ont_hi_ok"), sem("ont_lo_ok")
        wo_ok, h2_ok = sem("wo_ok"), sem("h2_ok")
        block = ctx.enter_context(nc.Block())

        def steps(eng, step):
            def straight(b):
                step(b, lambda n: (b + n) // 2, b % 2, [0 <= b + n < BATCH for n in (3, 2, 1, 0, -1, -2)])
            for b in range(-3, 3):
                straight(b)
            with eng.Fori(0, (BATCH - 6) // 2) as k:
                for c in (3, 4):
                    step(Count(k, 2, c), lambda n, c=c: Count(k, 1, (c + n) // 2), c % 2, [True] * 6)
            for b in range(BATCH - 3, BATCH + 2):
                straight(b)

        @block.sync
        def _(sp):
            def load(dst, ld, b, par):
                sp.dma_start(dst[par][0:PATCHES, :], emb[bass.ds(val(b * PATCHES), PATCHES), :]).then_inc(ld[par], 16)
                sp.dma_start(dst[par][PATCHES:T, :], txt[bass.ds(val(b * WORDS), WORDS), :]).then_inc(ld[par], 16)

            for b in range(2):
                load(h_in, h_ld, b, b)
            sp.dma_start(cos[:], rope_cos).then_inc(tables_in, 16)
            sp.dma_start(sin[:], rope_sin).then_inc(tables_in, 16)

            def step(b, half, par, flags):
                normalises, projects, turns, scores, finishes, adds = flags
                if normalises and (not isinstance(b, int) or b + 5 < BATCH):
                    sp.wait_ge(xn_ok, val(b + 4))
                    load(h_in, h_ld, b + 5, 1 - par)
                if adds:
                    sp.wait_ge(h2_ok, val(b - 1))
                    sp.dma_start(h2[bass.ds(val((b - 2) * T), T), :], h_out[par][:]).then_inc(h2_out[par], 16)
                if scores:
                    load(h_res, hr_ld, b, par)

            for b in range(-3, 3):
                step(b, None, b % 2, [0 <= b + n < BATCH for n in (3, 2, 1, 0, -1, -2)])
            with sp.Fori(0, (BATCH - 8) // 2) as k:
                for c in (3, 4):
                    step(Count(k, 2, c), None, c % 2, [True] * 6)
            for b in range(BATCH - 5, BATCH + 2):
                step(b, None, b % 2, [0 <= b + n < BATCH for n in (3, 2, 1, 0, -1, -2)])
            for i in range(2):
                sp.wait_ge(h2_out[i], 16 * (BATCH // 2))

        @block.vector
        def _(dve):
            nc.vector.memset(eps[:], EPS)
            nc.vector.memset(power[:], -0.5).then_inc(consts, 1)
            for i in range(2):
                nc.vector.memset(vp[i][:], 0.0).then_inc(values_clear, 1)
            dve.wait_ge(values_clear, 2)
            for i in range(2):
                nc.vector.memset(vp[i][:, :, DH:DH + 1], 1.0).then_inc(pads_ok, 1)
            for i in range(2):
                nc.vector.memset(kt[i][:].bitcast(F32), 0.0).then_inc(pads_ok, 1)

            def softmax_in(b, g):
                dve.wait_ge(score_ok, val(GROUPS * b + g + 1))
                nc.vector.reduce_max(smax[:, g % 2], p_score[g % 2][:, :, 0:T], AX_X).then_inc(max_ok, 1)
                dve.wait_ge(max_ok, val(GROUPS * b + g + 1))
                if g >= 2:
                    dve.wait_ge(pt_ps_ok, val(GROUPS * b + g - 1))
                elif not isinstance(b, int) or b >= 1:
                    dve.wait_ge(pt_ps_ok, val(GROUPS * b + g - 1))
                nc.vector.tensor_tensor(prob[g % 2][:], p_score[g % 2][:, :, 0:T],
                                        smax[:, g % 2].unsqueeze(2).broadcast_to([T, GH, T]),
                                        ALU.subtract).then_inc(sub_ok, 1)

            def step(b, half, par, flags):
                normalises, projects, turns, scores, finishes, adds = flags
                if scores:
                    softmax_in(b, 0)
                if scores:
                    softmax_in(b, 1)
                if adds:
                    dve.wait_ge(wo_ok, val(b - 1))
                    dve.wait_ge(hr_ld[par], val(32 * (half(-2) + 1)))
                    if not isinstance(b, int) or b >= 4:
                        dve.wait_ge(h2_out[par], val(16 * half(-2)))
                    nc.vector.tensor_tensor(h_out[par][:], p_v[:, 1, :], h_res[par][:], ALU.add).then_inc(h2_ok, 1)
                if projects:
                    dve.wait_ge(xt_hi_ok, val(b + 3))
                    nc.vector.tensor_tensor(xt_lo[par][:], xt_ps, xt_hi[par][:].bitcast(F32),
                                            ALU.subtract).then_inc(xt_lo_ok, 1)
                if scores:
                    softmax_in(b, 2)
                if normalises:
                    dve.wait_ge(h_ld[1 - par], val(32 * (half(3) + 1)))
                    nc.vector.bn_stats(stats[:], h_in[1 - par][:]).then_inc(stats_ok, 1)
                    dve.drain()
                    nc.vector.bn_aggr(mv[:], stats[:]).then_inc(mv_ok, 1)
                if scores:
                    softmax_in(b, 3)
                if finishes:
                    o_ps = p_misc[0:T, :].rearrange("p (g j d) -> p g j d", g=GROUPS, j=GH)
                    dve.wait_ge(o_ps_ok, val(b))
                    nc.vector.reciprocal(rz[:], o_ps[:, :, :, DH]).then_inc(rz_ok, 1)
                    dve.wait_ge(rz_ok, val(b))
                    if not isinstance(b, int) or b >= 2:
                        dve.wait_ge(ont_ps_ok, val(b - 1))
                    nc.vector.tensor_tensor(on[:], o_ps[:, :, :, 0:DH],
                                            rz[:].unsqueeze(3).broadcast_to([T, GROUPS, GH, DH]),
                                            ALU.mult).then_inc(on_ok, 1)
                if normalises:
                    dve.wait_ge(rstd_ok, val(b + 4))
                    if not isinstance(b, int) or b >= -1:
                        dve.wait_ge(xt_ps_ok, val(b + 2))
                    nc.vector.tensor_scalar(xn[1 - par][:], h_in[1 - par][:], mv[:, 0:1], rstd[:], ALU.subtract,
                                            ALU.mult).then_inc(xn_ok, 1)
                if projects:
                    dve.wait_ge(tables_in, 32)
                    dve.wait_ge(qk_ok, val(b + 3))
                    if not isinstance(b, int) or b >= -1:
                        dve.wait_ge(turned_ok, val(b + 2))
                    qk3 = p_qk[:].rearrange("p (h d) -> p h d", d=DH)
                    nc.vector.tensor_tensor(rope_a[:], qk3, cos[:].unsqueeze(1).broadcast_to([T, 2 * HEADS, DH]),
                                            ALU.mult)
                    for e in range(2):
                        last = nc.vector.tensor_tensor(
                            rope_b[:].rearrange("p h (i e) -> p h i e", e=2)[:, :, :, e],
                            qk3.rearrange("p h (i e) -> p h i e", e=2)[:, :, :, 1 - e],
                            sin[:].rearrange("p (i e) -> p i e", e=2)[:, :, e].unsqueeze(1).broadcast_to(
                                [T, 2 * HEADS, DH // 2]), ALU.mult)
                    last.then_inc(rope_ok, 1)
                if finishes:
                    dve.wait_ge(ont_hi_ok, val(b))
                    nc.vector.tensor_tensor(ont_lo[:], xt_ps, ont_hi[:].bitcast(F32), ALU.subtract).then_inc(ont_lo_ok, 1)

            steps(dve, step)

        @block.gpsimd
        def _(pool):
            for i in range(2):
                nc.gpsimd.memset(stack[i][:], 0.0).then_inc(stack_clear, 1)
                nc.gpsimd.memset(qt[i][:].bitcast(F32), 0.0).then_inc(q_clear, 1)
            pool.wait_ge(consts, 1)
            pool.wait_ge(stack_clear, 2)

            def step(b, half, par, flags):
                normalises, projects, turns, scores, finishes, adds = flags
                if normalises:
                    pool.wait_ge(mv_ok, val(b + 4))
                    nc.gpsimd.tensor_tensor(mv[:, 1:2], mv[:, 1:2], eps[:], ALU.add).then_inc(var_ok, 1)
                    pool.wait_ge(var_ok, val(b + 4))
                    nc.gpsimd.tensor_tensor(rstd[:], mv[:, 1:2], power[:], ALU.pow).then_inc(rstd_ok, 1)
                if projects:
                    pool.wait_ge(rope_ok, val(b + 3))
                    if not isinstance(b, int) or b >= -1:
                        pool.wait_ge(hi_ok, val(2 * (b + 2)))
                    nc.gpsimd.tensor_tensor(turned[:], rope_a[:], rope_b[:], ALU.add).then_inc(turned_ok, 1)
                    for s, slot in ((0, 2), (1, 1)):
                        pool.wait_ge(hi_ok, val(2 * (b + 2) + s + 1))
                        nc.gpsimd.tensor_tensor(stack[par][:, s, :, slot * DH:(slot + 1) * DH].bitcast(F32R),
                                                turned[:, s * HEADS:(s + 1) * HEADS, :],
                                                stack[par][:, s, :, 0:DH], ALU.subtract).then_inc(lo_ok, 1)

            steps(pool, step)
            pool.wait_ge(lo_ok, 2 * BATCH)

        @block.scalar
        def _(act):
            act.wait_ge(pads_ok, 4)
            act.wait_ge(q_clear, 2)
            act.wait_ge(stack_clear, 2)

            def exp_group(b, g):
                act.wait_ge(sub_ok, val(GROUPS * b + g + 1))
                nc.scalar.activation(prob[g % 2][:], prob[g % 2][:], ACT.Exp, scale=DH ** -0.5).then_inc(exp_ok, 1)

            def keep_prob_t(b, g):
                act.wait_ge(pt_ps_ok, val(GROUPS * b + g + 1))
                if g >= 2 or not isinstance(b, int) or b >= 1:
                    act.wait_ge(pv_ok, val(GROUPS * b + g - 1))
                nc.scalar.activation(prob_t[g % 2][:], p_turn[g % 2][0:T], ACT.Copy).then_inc(pt_ok, 1)

            def keep_qkt(b, par, n):
                act.wait_ge(qkt_ps_ok, val(4 * (b + 1) + n + 1))
                if n == 0 and (not isinstance(b, int) or b >= 1):
                    act.wait_ge(score_ok, val(GROUPS * b))
                dst = (qt if n < 2 else kt)[1 - par]
                nc.scalar.activation(dst[:, 4 * (n % 2):4 * (n % 2) + 4, 0:T], p_turn[n % 2][:], ACT.Copy).then_inc(qkt_ok, 1)

            def step(b, half, par, flags):
                normalises, projects, turns, scores, finishes, adds = flags
                if scores:
                    exp_group(b, 0)
                if projects and (not isinstance(b, int) or b >= -2):
                    act.wait_ge(xt_ps_ok, val(b + 3))
                    if not isinstance(b, int) or b >= 0:
                        act.wait_ge(v_ps_ok, val(b + 1))
                    nc.scalar.activation(xt_hi[par][:], xt_ps, ACT.Copy).then_inc(xt_hi_ok, 1)
                if scores:
                    exp_group(b, 1)
                    keep_prob_t(b, 0)
                    exp_group(b, 2)
                    keep_prob_t(b, 1)
                    exp_group(b, 3)
                if turns:
                    act.wait_ge(v_ps_ok, val(b + 2))
                    if not isinstance(b, int) or b >= 1:
                        act.wait_ge(pv_ok, val(GROUPS * b))
                    nc.scalar.activation(vp[1 - par][:, :, 0:DH], p_v[:, 0, :].rearrange("p (h d) -> p h d", d=DH),
                                         ACT.Copy).then_inc(v_ok, 1)
                    keep_qkt(b, par, 0)
                    keep_qkt(b, par, 1)
                if scores:
                    keep_prob_t(b, 2)
                    keep_prob_t(b, 3)
                if finishes:
                    act.wait_ge(ont_ps_ok, val(b))
                    if not isinstance(b, int) or b >= 2:
                        act.wait_ge(wo_ok, val(b - 1))
                    nc.scalar.activation(ont_hi[:], xt_ps, ACT.Copy).then_inc(ont_hi_ok, 1)
                if turns:
                    keep_qkt(b, par, 2)
                    keep_qkt(b, par, 3)
                if scores:
                    act.wait_ge(pv_ok, val(GROUPS * (b + 1)))
                    if not isinstance(b, int) or b >= 1:
                        act.wait_ge(o_ps_ok, val(b))
                    nc.scalar.activation(ot_sb[:], p_ot[:], ACT.Copy).then_inc(ot_ok, 1)
                if projects:
                    act.wait_ge(turned_ok, val(b + 3))
                    if not isinstance(b, int) or b >= 0:
                        act.wait_ge(qkt_ps_ok, val(4 * (b + 1)))
                    for s, step_ in ((0, 1), (1, 2)):
                        dst = stack[par][:, s].rearrange("p h (r d) -> p h r d", d=DH)[:, :, 0:step_ + 1:step_, :]
                        src = turned[:, s * HEADS:(s + 1) * HEADS, :].unsqueeze(2).broadcast_to([T, HEADS, 2, DH])
                        nc.scalar.activation(dst.bitcast(F32R), src, ACT.Copy).then_inc(hi_ok, 1)

            steps(act, step)

        @block.tensor
        def _(pe):
            pe.wait_ge(pads_ok, 4)

            def score(b, par, g):
                if g >= 2 or not isinstance(b, int) or b >= 1:
                    pe.wait_ge(sub_ok, val(GROUPS * b + g - 1))
                base = 64 * (g % 2)
                for j in range(GH):
                    h = head_of(g, j)
                    last = nc.tensor.matmul(p_score[g % 2][:, j, :], qt[par][base:base + 3 * DH, h // 2, 0:T],
                                            kt[par][base:base + 3 * DH, h // 2, :], start=True, stop=True)
                last.then_inc(score_ok, 1)

            def turn_probs(b, g):
                pe.wait_ge(exp_ok, val(GROUPS * b + g + 1))
                for j in range(GH):
                    last = nc.tensor.transpose(p_turn[g % 2][0:T, j, :], prob[g % 2][:, j, :], ident[0:T, 0:T])
                last.then_inc(pt_ps_ok, 1)

            def weigh_values(b, par, g):
                pe.wait_ge(pt_ok, val(GROUPS * b + g + 1))
                for j in range(GH):
                    last = nc.tensor.matmul(p_ot[32 * j:32 * j + 32, g, :], vp[par][:, head_of(g, j), :],
                                            prob_t[g % 2][:, j, :], start=True, stop=True)
                last.then_inc(pv_ok, 1)

            def turn_qk(b, par, n):
                for i in range(4):
                    hp = 4 * (n % 2) + i
                    last = nc.tensor.transpose(p_turn[n % 2][:, i, :],
                                               stack[1 - par][:, n // 2, 2 * hp:2 * hp + 2, :], ident[0:T, 0:T])
                last.then_inc(qkt_ps_ok, 1)

            def split_product(out, hi, lo, w_hi, w_lo):
                n = 0
                for a, w in ((hi, w_hi), (hi, w_lo), (lo, w_hi)):
                    for k in range(KC):
                        last = nc.tensor.matmul(out, a[:, k, :], w[:, k, :], start=n == 0, stop=n == 3 * KC - 1)
                        n += 1
                return last

            def step(b, half, par, flags):
                normalises, projects, turns, scores, finishes, adds = flags
                first = isinstance(b, int)
                if scores:
                    pe.wait_ge(qkt_ok, val(4 * b + 3))
                    score(b, par, 0)
                if scores:
                    score(b, par, 1)
                if projects:
                    pe.wait_ge(xn_ok, val(b + 3))
                    if not first or b >= 2:
                        pe.wait_ge(ont_lo_ok, val(b - 1))
                    elif b >= -1:
                        pe.wait_ge(xt_lo_ok, val(b + 2))
                    for k in range(KC):
                        last = nc.tensor.transpose(xt_ps[:, k, :], xn[par][:, 128 * k:128 * k + 128], ident[0:T, 0:T])
                    last.then_inc(xt_ps_ok, 1)
                if adds:
                    pe.wait_ge(ont_lo_ok, val(b - 1))
                    if scores:
                        pe.wait_ge(v_ok, val(b + 1))
                    elif b >= 3:
                        pe.wait_ge(h2_ok, b - 2)
                    split_product(p_v[:, 1, :], ont_hi, ont_lo, wo_hi, wo_lo).then_inc(wo_ok, 1)
                if scores:
                    pe.wait_ge(qkt_ok, val(4 * (b + 1)))
                    score(b, par, 2)
                    turn_probs(b, 0)
                    score(b, par, 3)
                    turn_probs(b, 1)
                if turns:
                    if not first or b >= 2:
                        pe.wait_ge(h2_ok, val(b - 1))
                    if not first or b >= 0:
                        pe.wait_ge(v_ok, val(b + 1))
                    split_product(p_v[:, 0, :], xt_hi[1 - par], xt_lo[1 - par], wv_hi, wv_lo).then_inc(v_ps_ok, 1)
                if finishes:
                    pe.wait_ge(ot_ok, val(b))
                    if projects:
                        pe.wait_ge(xt_lo_ok, val(b + 3))
                    elif b >= 2:
                        pe.wait_ge(ont_lo_ok, val(b - 1))
                    for g in range(GROUPS):
                        last = nc.tensor.transpose(p_misc[0:T, 128 * g:128 * g + 128], ot_sb[:, g, :], ident[:, :])
                    last.then_inc(o_ps_ok, 1)
                if turns:
                    pe.wait_ge(lo_ok, val(2 * (b + 2)))
                    for n in range(2):
                        if scores:
                            pe.wait_ge(pt_ok, val(GROUPS * b + n + 1))
                        turn_qk(b, par, n)
                if scores:
                    if not first or b >= 1:
                        pe.wait_ge(ot_ok, val(b))
                    pe.wait_ge(v_ok, val(b + 1))
                    weigh_values(b, par, 0)
                    weigh_values(b, par, 1)
                if projects:
                    pe.wait_ge(xt_lo_ok, val(b + 3))
                    if not first or b >= -1:
                        pe.wait_ge(rope_ok, val(b + 2))
                    split_product(p_qk[:], xt_hi[par], xt_lo[par], wqk_hi, wqk_lo).then_inc(qk_ok, 1)
                if scores:
                    for n in range(2):
                        if turns:
                            pe.wait_ge(qkt_ok, val(4 * (b + 1) + n + 1))
                        turn_probs(b, 2 + n)
                if finishes:
                    pe.wait_ge(on_ok, val(b))
                    for k in range(KC):
                        last = nc.tensor.transpose(xt_ps[:, k, :], on[:].rearrange("p g j d -> p (g j d)")[:, 128 * k:128 * k + 128],
                                                   ident[0:T, 0:T])
                    last.then_inc(ont_ps_ok, 1)
                if scores:
                    weigh_values(b, par, 2)
                if turns:
                    if scores:
                        pe.wait_ge(pt_ok, val(GROUPS * b + 3))
                    else:
                        pe.wait_ge(qkt_ok, val(4 * (b + 1) + 1))
                    turn_qk(b, par, 2)
                if scores:
                    weigh_values(b, par, 3)
                if turns:
                    if scores:
                        pe.wait_ge(pt_ok, val(GROUPS * (b + 1)))
                    else:
                        pe.wait_ge(qkt_ok, val(4 * (b + 1) + 2))
                    turn_qk(b, par, 3)

            steps(pe, step)


def dispatch(nc, h2, phi, slot_bias, ident, xacc, ct_out, ebias, eb, eb_in, wexp, w_slots, w_in):
    phi_hi, phi_lo = phi
    bias_rows, bias_ones = slot_bias
    with ExitStack() as ctx:
        sb = lambda name, shape, dt=F32: ctx.enter_context(nc.sbuf_tensor(f"dispatch_{name}", shape, dt))
        pb = lambda name, shape: ctx.enter_context(nc.psum_tensor(f"dispatch_{name}", shape, F32))
        sem = lambda name: ctx.enter_context(nc.semaphore(f"dispatch_{name}"))
        RING = 2 * TG
        h_t = [sb(f"h_t{i}", [128, C]) for i in range(2)]
        xn = [sb(f"xn{i}", [128, C]) for i in range(2)]
        x = [sb(f"x{i}", [128, C]) for i in range(RING)]
        stats, mv, rstd, power = sb("stats", [128, 6]), sb("mv", [128, 2]), sb("rstd", [128, 1]), sb("power", [128, 1])
        eps = sb("eps", [128, 1])
        xt_hi, xt_lo = sb("xt_hi", [128, KC, 128], F32R), sb("xt_lo", [128, KC, 128], F32R)
        dmax, cmax = sb("dmax", [128, EXPERTS]), sb("cmax", [128, SLOTS])
        dsum, csum = sb("dsum", [128, 2, EXPERTS]), sb("csum", [128, 2, SLOTS])
        disp = [sb(f"disp{i}", [128, EXPERTS, SLOTS]) for i in range(RING)]
        comb = [sb(f"comb{i}", [128, EXPERTS, SLOTS]) for i in range(2)]
        ct = [sb(f"ct{i}", [128, EB, 128]) for i in range(2)]

        logits = pb("logits", [128, EXPERTS, SLOTS])
        p_turn = [pb(f"p_turn{i}", [128, 4, 128]) for i in range(2)]
        p_sum = [pb(f"p_sum{i}", [128, 2, C]) for i in range(2)]
        NB = 4
        XB = EXPERTS // NB
        bank = lambda c: slice(c * XB, (c + 1) * XB)

        consts = sem("consts")
        h_ld, ct_st = [sem("h_ld0"), sem("h_ld1")], [sem("ct_st0"), sem("ct_st1")]
        stats_ok, mv_ok, var_ok, rstd_ok, x_ok = sem("stats_ok"), sem("mv_ok"), sem("var_ok"), sem("rstd_ok"), sem("x_ok")
        xt_ps_ok, xt_hi_ok, xt_lo_ok = sem("xt_ps_ok"), sem("xt_hi_ok"), sem("xt_lo_ok")
        logit_ok, dmax_ok, dsub_ok, cmax_ok, csub_ok = sem("logit_ok"), sem("dmax_ok"), sem("dsub_ok"), sem("cmax_ok"), sem("csub_ok")
        dexp_ok, cexp_ok, dsum_ok, csum_ok = sem("dexp_ok"), sem("cexp_ok"), sem("dsum_ok"), sem("csum_ok")
        drec_ok, crec_ok, disp_ok, comb_ok = sem("drec_ok"), sem("crec_ok"), sem("disp_ok"), sem("comb_ok")
        kept_ok, copied_ok = sem("kept_ok"), sem("copied_ok")
        ct_ps_ok, ct_ok, sum_ok, acc_ok = sem("ct_ps_ok"), sem("ct_ok"), sem("sum_ok"), sem("acc_ok")
        block = ctx.enter_context(nc.Block())
        UNITS = EB // 2
        PER = UNITS // TG

        def steps(eng, step):
            straight = lambda t: step(t, lambda n: (t + n) // 2, t, TAIL if t == FULL_TILES else 128)
            for t in range(-2, TG):
                straight(t)
            with eng.Fori(0, (FULL_TILES - TG) // RING) as k:
                for c in range(TG, TG + RING):
                    step(Count(k, RING, c), lambda n, c=c: Count(k, TG, (c + n) // 2), c, 128)
            straight(FULL_TILES)
            straight(FULL_TILES + 1)

        static = lambda t: isinstance(t, int)

        last_tile = lambda t: static(t) and t == FULL_TILES

        def flags(t):
            if not static(t):
                return True, True, True, 128
            return 0 <= t < TILES, 0 <= t + 1 < TILES, t + 2 < TILES, TAIL if t + 1 == FULL_TILES else 128

        def products_of(n, xc):
            return PER * (n - xc % TG) - UNITS

        def sums(t, c):
            if not static(t):
                return [(2 * t - UNITS + i, PER * (c % TG) + i) for i in range(PER)]
            if t < TG:
                return []
            g = FULL_TILES // TG - 1 + t - FULL_TILES
            return [(UNITS * g + u, u) for u in range(UNITS)]

        @block.sync
        def _(sp):
            def load(t, par, rows=128):
                sp.dma_start(h_t[par][0:rows], h2[bass.ds(val(t * 128), rows), :]).then_inc(h_ld[par], 16)

            load(0, 0)
            load(1, 1)
            for j in range(EPB):
                sp.dma_start(eb[SLOTS * j:SLOTS * (j + 1)], ebias[j:j + 1].broadcast_to([SLOTS, EB, C])).then_inc(eb_in, 16)

            def store(t, par, rows):
                for q in range(4):
                    sp.wait_ge(ct_ok, val(4 * t + q + 1))
                    sp.dma_start(ct_out[bass.ds(val(t * 128), 128), 4 * q:4 * q + 4, 0:rows],
                                 ct[par][:, 4 * q:4 * q + 4, 0:rows]).then_inc(ct_st[par], 16)

            def step(t, half, c, rows):
                if not static(t) or t + 3 <= TILES:
                    sp.wait_ge(x_ok, val(t + 2))
                    if not static(t) or t + 3 < TILES:
                        load(t + 3, (c + 3) % 2, TAIL if static(t) and t + 3 == FULL_TILES else 128)
                    else:
                        load(0, TILES % 2)
                if not static(t) or t >= 1:
                    store(t - 1, (c + 1) % 2,
                          TAIL if static(t) and t - 1 == FULL_TILES else 128)

            for t in range(-1, TG):
                step(t, None, t, 128)
            with sp.Fori(0, (FULL_TILES - 2 * TG) // TG) as k:
                for c in range(TG, 2 * TG):
                    step(Count(k, TG, c), None, c, 128)
            for t in range(FULL_TILES - TG, FULL_TILES + 2):
                if t == FULL_TILES:
                    sp.wait_ge(logit_ok, NB * TILES)
                    for i, slot in enumerate(w_slots):
                        sp.dma_start(slot, wexp[i]).then_inc(w_in[i], 16)
                step(t, None, t, 128)
            sp.wait_ge(ct_st[0], 64 * ((TILES + 1) // 2))
            sp.wait_ge(ct_st[1], 64 * (TILES // 2))

        @block.vector
        def _(dve):
            nc.vector.memset(eps[:], EPS)
            nc.vector.memset(power[:], -0.5).then_inc(consts, 1)

            def norm(n, par, xc, rows, half):
                dve.wait_ge(h_ld[par], val(16 * (half + 1)))
                nc.vector.bn_stats(stats[0:rows], h_t[par][0:rows]).then_inc(stats_ok, 1)
                dve.drain()
                nc.vector.bn_aggr(mv[0:rows], stats[0:rows]).then_inc(mv_ok, 1)

            def norm_end(n, par, xc, rows):
                dve.wait_ge(rstd_ok, val(n + 1))
                if not static(n) or n >= 2:
                    dve.wait_ge(kept_ok, val(n - 1))
                    dve.wait_ge(xt_ps_ok, val(n - 1))
                nc.vector.tensor_scalar(xn[xc % 2][0:rows], h_t[par][0:rows], mv[0:rows, 0:1], rstd[0:rows],
                                        ALU.subtract, ALU.mult).then_inc(x_ok, 1)

            def keep_sum(s, u):
                dve.wait_ge(sum_ok, val(s + 1))
                nc.vector.tensor_tensor(xacc[:, 2 * u:2 * u + 2, :], p_sum[u % 2][:], xacc[:, 2 * u:2 * u + 2, :],
                                        ALU.add).then_inc(acc_ok, 1)

            def combine_sum(n, par, rows):
                dve.wait_ge(cexp_ok, val(2 * (n + 1)))
                if not static(n) or n >= 1:
                    dve.wait_ge(comb_ok, val(n))
                nc.vector.reduce_sum(csum[0:rows, 0], comb[par % 2][0:rows].rearrange("p n s -> p s n"), AX_X).then_inc(csum_ok, 1)
                dve.wait_ge(csum_ok, val(n + 1))
                nc.vector.reciprocal(csum[0:rows, 1], csum[0:rows, 0]).then_inc(crec_ok, 1)

            def step(t, half, c, rows):
                live, nxt, ahead, nrows = flags(t)

                def dispatch_in(b):
                    dve.wait_ge(logit_ok, val(NB * t + b + 1))
                    nc.vector.reduce_max(dmax[0:rows, bank(b)], logits[0:rows, bank(b), :], AX_X).then_inc(dmax_ok, 1)
                    dve.wait_ge(dmax_ok, val(NB * t + b + 1))
                    if b == 0 and (not static(t) or t >= RING):
                        dve.wait_ge(acc_ok, val(products_of(t, c) + 2))
                    nc.vector.tensor_tensor(disp[c % RING][0:rows, bank(b), :], logits[0:rows, bank(b), :],
                                            dmax[0:rows, bank(b)].unsqueeze(2).broadcast_to([rows, XB, SLOTS]),
                                            ALU.subtract).then_inc(dsub_ok, 1)

                if live:
                    dispatch_in(0)
                    dispatch_in(1)
                if not static(t) or 1 <= t <= FULL_TILES:
                    combine_sum(t - 1, c + 1, 128)
                if nxt:
                    dve.wait_ge(xt_hi_ok, val(t + 2))
                    nc.vector.tensor_tensor(xt_lo[:, :, 0:nrows], p_turn[0][:, 0:KC, 0:nrows],
                                            xt_hi[:, :, 0:nrows].bitcast(F32), ALU.subtract).then_inc(xt_lo_ok, 1)
                if live:
                    dispatch_in(2)
                    dispatch_in(3)
                if ahead:
                    norm(t + 2, c % 2, c + 2, 128 if not static(t) or t + 2 < FULL_TILES else TAIL, half(2))
                if live:
                    dve.wait_ge(copied_ok, val(NB * (t + 1)))
                    if not static(t) or t >= 1:
                        dve.wait_ge(csub_ok, val(2 * t))
                    nc.vector.reduce_max(cmax[0:rows], comb[c % 2][0:rows].rearrange("p n s -> p s n"), AX_X).then_inc(cmax_ok, 1)
                if ahead:
                    norm_end(t + 2, c % 2, c + 2, 128)
                if live:
                    dve.wait_ge(dexp_ok, val(2 * (t + 1)))
                    if not static(t) or t >= 1:
                        dve.wait_ge(disp_ok, val(t))
                    nc.vector.reduce_sum(dsum[0:rows, 0], disp[c % RING][0:rows], AX_X).then_inc(dsum_ok, 1)
                    dve.wait_ge(dsum_ok, val(t + 1))
                    nc.vector.reciprocal(dsum[0:rows, 1], dsum[0:rows, 0]).then_inc(drec_ok, 1)
                for s, u in sums(t, c)[:PER if last_tile(t) else None]:
                    keep_sum(s, u)
                if last_tile(t):
                    combine_sum(t, c, TAIL)
                    for s, u in sums(t, c)[PER:]:
                        keep_sum(s, u)

            steps(dve, step)

        @block.gpsimd
        def _(pool):
            for i in range(2):
                nc.gpsimd.memset(xacc[:, i * EB // 2:(i + 1) * EB // 2, :], 0.0).then_inc(acc_ok, 1)
            pool.wait_ge(consts, 1)

            def step(t, half, c, rows):
                live, nxt, ahead, nrows = flags(t)
                if ahead:
                    nrows = TAIL if static(t) and t + 2 == FULL_TILES else 128
                    pool.wait_ge(mv_ok, val(t + 3))
                    nc.gpsimd.tensor_tensor(mv[0:nrows, 1:2], mv[0:nrows, 1:2], eps[0:nrows], ALU.add).then_inc(var_ok, 1)
                    pool.wait_ge(var_ok, val(t + 3))
                    nc.gpsimd.tensor_tensor(rstd[0:nrows], mv[0:nrows, 1:2], power[0:nrows], ALU.pow).then_inc(rstd_ok, 1)
                if live:
                    pool.wait_ge(cmax_ok, val(t + 1))
                    for i in range(2):
                        m = comb[c % 2][0:rows, 2 * i * XB:2 * (i + 1) * XB, :]
                        nc.gpsimd.tensor_tensor(m, m, cmax[0:rows].unsqueeze(1).broadcast_to([rows, 2 * XB, SLOTS]),
                                                ALU.subtract).then_inc(csub_ok, 1)
                    pool.wait_ge(drec_ok, val(t + 1))
                    d = disp[c % RING][0:rows]
                    nc.gpsimd.tensor_tensor(d, d, dsum[0:rows, 1].unsqueeze(2).broadcast_to([rows, EXPERTS, SLOTS]),
                                            ALU.mult).then_inc(disp_ok, 1)
                    pool.wait_ge(crec_ok, val(t + 1))
                    m = comb[c % 2][0:rows]
                    nc.gpsimd.tensor_tensor(m, m, csum[0:rows, 1].unsqueeze(1).broadcast_to([rows, EXPERTS, SLOTS]),
                                            ALU.mult).then_inc(comb_ok, 1)

            steps(pool, step)

        @block.scalar
        def _(act):
            def step(t, half, c, rows):
                live, nxt, ahead, nrows = flags(t)
                prow = TAIL if static(t) and t - 1 == FULL_TILES else 128

                def exp_half(buf, before, per, done, i):
                    act.wait_ge(before, val(2 * per * t + per * (i + 1)))
                    part = buf[0:rows, 2 * i * XB:2 * (i + 1) * XB, :]
                    nc.scalar.activation(part, part, ACT.Exp).then_inc(done, 1)

                def keep_quarter(q):
                    act.wait_ge(ct_ps_ok, val(4 * (t - 1) + q + 1))
                    if q == 0 and (not static(t) or t >= 3):
                        act.wait_ge(ct_st[(c + 1) % 2], val(64 * half(-1)))
                    nc.scalar.activation(ct[(c + 1) % 2][:, 4 * q:4 * q + 4, 0:prow], p_turn[q % 2][:, :, 0:prow],
                                         ACT.Copy).then_inc(ct_ok, 1)

                if live:
                    act.wait_ge(x_ok, val(t + 1))
                    if not static(t) or t >= RING:
                        act.wait_ge(acc_ok, val(products_of(t, c) + 2))
                    nc.scalar.activation(x[c % RING][0:rows], xn[c % 2][0:rows], ACT.Copy).then_inc(kept_ok, 1)
                if nxt:
                    act.wait_ge(xt_ps_ok, val(t + 2))
                    nc.scalar.activation(xt_hi[:, :, 0:nrows], p_turn[0][:, 0:KC, 0:nrows], ACT.Copy).then_inc(xt_hi_ok, 1)
                if live:
                    if not static(t) or t >= 2:
                        act.wait_ge(ct_ps_ok, val(4 * (t - 1)))
                    for b in range(NB):
                        act.wait_ge(dsub_ok, val(NB * t + b + 1))
                        nc.scalar.activation(comb[c % 2][0:rows, bank(b), :], logits[0:rows, bank(b), :],
                                             ACT.Copy).then_inc(copied_ok, 1)
                if live:
                    exp_half(disp[c % RING], dsub_ok, 2, dexp_ok, 0)
                    exp_half(disp[c % RING], dsub_ok, 2, dexp_ok, 1)
                if not static(t) or t >= 1:
                    for q in range(0, 4):
                        keep_quarter(q)
                if live:
                    exp_half(comb[c % 2], csub_ok, 1, cexp_ok, 0)
                    exp_half(comb[c % 2], csub_ok, 1, cexp_ok, 1)

            steps(act, step)

        @block.tensor
        def _(pe):
            def turn_x(t, c, nrows):
                pe.wait_ge(x_ok, val(t + 2))
                if not static(t) or t >= 2:
                    pe.wait_ge(ct_ok, val(4 * (t - 2) + 3))
                for k in range(KC):
                    last = nc.tensor.transpose(p_turn[0][:, k, 0:nrows], xn[(c + 1) % 2][0:nrows, 128 * k:128 * k + 128],
                                               ident[0:nrows, 0:nrows])
                last.then_inc(xt_ps_ok, 1)

            def turn_weights(t, c, q):
                prow = TAIL if static(t) and t - 1 == FULL_TILES else 128
                flat = comb[(c + 1) % 2][0:prow].rearrange("p n s -> p (n s)")
                if q == 0:
                    pe.wait_ge(comb_ok, val(t))
                    if not static(t) or t + 1 < TILES:
                        pe.wait_ge(xt_lo_ok, val(t + 2))
                if (q > 0 or static(t) and t + 1 >= TILES) and (not static(t) or 4 * (t - 1) + q - 1 > 0):
                    pe.wait_ge(ct_ok, val(4 * (t - 1) + q - 1))
                for i in range(4):
                    e = 4 * q + i
                    last = nc.tensor.transpose(p_turn[q % 2][:, i, 0:prow], flat[:, 128 * e:128 * e + 128],
                                               ident[0:prow, 0:prow])
                last.then_inc(ct_ps_ok, 1)

            def multiply_group(t, c, units):
                tail = static(t) and t == FULL_TILES + 1
                if tail:
                    tiles, n = [FULL_TILES % RING], TAIL
                else:
                    g = (c // TG + 1) % 2
                    tiles, n = range(TG * g, TG * g + TG), 128
                for s, u in units:
                    pe.wait_ge(disp_ok, val(FULL_TILES + 1 if tail else t - c % TG))
                    pe.wait_ge(kept_ok, val(FULL_TILES + 1 if tail else t - c % TG))
                    pe.wait_ge(acc_ok, val(s + 1))
                    for i in range(2):
                        e = 2 * u + i
                        for n_th, d in enumerate(tiles):
                            last = nc.tensor.matmul(p_sum[u % 2][:, i, :],
                                                    disp[d][0:n].rearrange("p n s -> p (n s)")[:, 128 * e:128 * e + 128],
                                                    x[d][0:n], start=n_th == 0, stop=n_th == len(tiles) - 1)
                    last.then_inc(sum_ok, 1)

            def multiply_logits(t, nrows):
                pe.wait_ge(xt_lo_ok, val(t + 2))
                for b in range(NB):
                    if not static(t) or t >= 0:
                        pe.wait_ge(copied_ok, val(NB * t + b + 1))
                    out = logits[0:nrows, bank(b), :]
                    cols = slice(512 * b, 512 * (b + 1))
                    nc.tensor.matmul(out, bias_ones[:, 0:nrows], bias_rows[:, cols], start=True, stop=False)
                    for i, (a, w) in enumerate(((xt_hi, phi_hi), (xt_hi, phi_lo), (xt_lo, phi_hi))):
                        for k in range(KC):
                            last = nc.tensor.matmul(out, a[:, k, 0:nrows], w[:, k, cols], start=False,
                                                    stop=i == 2 and k == KC - 1)
                    last.then_inc(logit_ok, 1)

            def step(t, half, c, rows):
                live, nxt, ahead, nrows = flags(t)
                units = sums(t, c)
                if nxt:
                    turn_x(t, c, nrows)
                multiply_group(t, c, units[:PER] if last_tile(t) else units)
                early = static(t) and t < TG
                if nxt and early:
                    multiply_logits(t, nrows)
                if not static(t) or t >= 1:
                    for q in range(4):
                        turn_weights(t, c, q)
                if last_tile(t):
                    multiply_group(t, c, units[PER:])
                if nxt and not early:
                    multiply_logits(t, nrows)

            steps(pe, step)


def experts(nc, xacc, wexp, w_slots, w_in, eb, eb_in, ident, y_hi, y_lo, ct_in, h2, combine_in):
    with ExitStack() as ctx:
        sb = lambda name, shape, dt=F32: ctx.enter_context(nc.sbuf_tensor(f"experts_{name}", shape, dt))
        pb = lambda name, shape: ctx.enter_context(nc.psum_tensor(f"experts_{name}", shape, F32))
        sem = lambda name: ctx.enter_context(nc.semaphore(f"experts_{name}"))
        RING, AHEAD = len(w_in), len(w_slots)
        w = w_slots + [sb(f"w{i}", [128, EPB, KC, C])[:] for i in range(AHEAD, RING)]
        raw, h_t, ld, h_ld = combine_in
        stats, mv, rstd = sb("stats", [128, EB, 6]), sb("mv", [128, EB, 2]), sb("rstd", [128, EB])
        power = sb("power", [128, EB])
        PARTS = [slice(0, EB // 4), slice(EB // 4, EB)]
        xs = xacc
        xst = [sb(f"xst{i}", [128, KC, 128]) for i in range(2)]
        y = sb("y", [128, 2, C])
        p_t = [pb(f"p_t{i}", [128, KC, 128]) for i in range(2)]
        p_y = [pb(f"p_y{i}", [128, C]) for i in range(2)]
        clip_ok, stats_ok, mv_ok, var_ok, rstd_ok = sem("clip_ok"), sem("stats_ok"), sem("mv_ok"), sem("var_ok"), sem("rstd_ok")
        consts, norm_ok, tanh_ok, t_ps_ok, t_ok = sem("consts"), sem("norm_ok"), sem("tanh_ok"), sem("t_ps_ok"), sem("t_ok")
        y_ps_ok, y_ok, hi_ok, lo_ok = sem("y_ps_ok"), sem("y_ok"), sem("hi_ok"), sem("lo_ok")
        block = ctx.enter_context(nc.Block())

        @block.sync
        def _(sp):
            for i in range(AHEAD, EB):
                if i >= RING:
                    sp.wait_ge(y_ps_ok, i - RING + 1)
                sp.dma_start(w[i % RING], wexp[i]).then_inc(w_in[i % RING], 16)
            for c in range(COMBINE_RING):
                sp.dma_start(raw[c][:], ct_in[c * 128:(c + 1) * 128]).then_inc(ld[c], 16)
                sp.dma_start(h_t[c][:], h2[c * 128:(c + 1) * 128, :]).then_inc(h_ld[c], 16)

        @block.vector
        def _(dve):
            nc.vector.memset(power[:], -0.5).then_inc(consts, 1)
            for p in PARTS:
                nc.vector.tensor_scalar(xacc[:, p], xacc[:, p], CLIP_LO, CLIP_HI, ALU.max, ALU.min).then_inc(clip_ok, 1)
            for n, p in enumerate(PARTS):
                dve.wait_ge(clip_ok, n + 1)
                for i in range(p.start, p.stop):
                    nc.vector.bn_stats(stats[:, i], xacc[:, i]).then_inc(stats_ok, 1)
                dve.wait_ge(stats_ok, p.stop)
                for i in range(p.start, p.stop):
                    nc.vector.bn_aggr(mv[:, i], stats[:, i]).then_inc(mv_ok, 1)
            for n, p in enumerate(PARTS):
                dve.wait_ge(rstd_ok, n + 1)
                for i in range(p.start, p.stop):
                    nc.vector.tensor_scalar(xs[:, i], xacc[:, i], mv[:, i, 0:1], rstd[:, i:i + 1], ALU.subtract,
                                            ALU.mult).then_inc(norm_ok, 1)
            dve.wait_ge(eb_in, 16 * EPB)
            for i in range(EB):
                dve.wait_ge(y_ps_ok, i + 1)
                if i >= 2:
                    dve.wait_ge(lo_ok, i - 1)
                nc.vector.tensor_tensor(y[:, i % 2], p_y[i % 2][:], eb[:, i], ALU.add).then_inc(y_ok, 1)

        @block.gpsimd
        def _(pool):
            pool.wait_ge(consts, 1)
            for n, p in enumerate(PARTS):
                pool.wait_ge(mv_ok, p.stop)
                nc.gpsimd.tensor_scalar(mv[:, p, 1], mv[:, p, 1], EPS, None, ALU.add).then_inc(var_ok, 1)
                pool.wait_ge(var_ok, n + 1)
                nc.gpsimd.tensor_tensor(rstd[:, p], mv[:, p, 1], power[:, p], ALU.pow).then_inc(rstd_ok, 1)
            for i in range(EB):
                pool.wait_ge(hi_ok, i + 1)
                nc.gpsimd.tensor_tensor(y_lo[:, i], y[:, i % 2], y_hi[:, i].bitcast(F32), ALU.subtract).then_inc(lo_ok, 1)
            pool.wait_ge(lo_ok, EB)

        @block.scalar
        def _(act):
            def tanh(i):
                act.wait_ge(norm_ok, i + 1)
                nc.scalar.activation(xs[:, i], xs[:, i], ACT.Tanh).then_inc(tanh_ok, 1)

            for i in range(EB):
                tanh(i)
            for i in range(EB + 1):
                if i < EB:
                    act.wait_ge(t_ps_ok, i + 1)
                    if i >= 2:
                        act.wait_ge(y_ps_ok, i - 1)
                    nc.scalar.activation(xst[i % 2][:], p_t[i % 2][:], ACT.Copy).then_inc(t_ok, 1)
                if i >= 1:
                    act.wait_ge(y_ok, i)
                    nc.scalar.activation(y_hi[:, i - 1], y[:, (i - 1) % 2], ACT.Copy).then_inc(hi_ok, 1)

        @block.tensor
        def _(pe):
            for i in range(EB + 1):
                if i < EB:
                    pe.wait_ge(tanh_ok, i + 1)
                    if i >= 2:
                        pe.wait_ge(t_ok, i - 1)
                    for k in range(KC):
                        last = nc.tensor.transpose(p_t[i % 2][:, k], xs[:, i, 128 * k:128 * k + 128], ident[:, :])
                    last.then_inc(t_ps_ok, 1)
                if i >= 1:
                    n = i - 1
                    pe.wait_ge(t_ok, n + 1)
                    pe.wait_ge(w_in[n % RING], 16 * (n // RING + 1))
                    if n >= 2:
                        pe.wait_ge(y_ok, n - 1)
                    for k in range(KC):
                        for j in range(EPB):
                            last = nc.tensor.matmul(p_y[n % 2][SLOTS * j:SLOTS * (j + 1), :],
                                                    xst[n % 2][:, k, SLOTS * j:SLOTS * (j + 1)],
                                                    w[n % RING][:, j, k, :], start=k == 0, stop=k == KC - 1)
                    last.then_inc(y_ps_ok, 1)


def combine(nc, ct_in, h2, y_hi, y_lo, combine_in, out):
    with ExitStack() as ctx:
        sb = lambda name, shape, dt=F32: ctx.enter_context(nc.sbuf_tensor(f"combine_{name}", shape, dt))
        sem = lambda name: ctx.enter_context(nc.semaphore(f"combine_{name}"))
        RING = COMBINE_RING
        raw, h_t, ld, h_ld = combine_in
        hi = [sb(f"hi{i}", [128, EB, 128], F32R) for i in range(2)]
        lo = [sb(f"lo{i}", [128, EB, 128], F32R) for i in range(2)]
        o = [sb(f"o{i}", [128, C]) for i in range(2)]
        p_o = [ctx.enter_context(nc.psum_tensor(f"combine_p_o{i}", [128, C], F32)) for i in range(2)]
        st = [sem("st0"), sem("st1")]
        hi_ok, lo_ok, mm_ok, o_ok = sem("hi_ok"), sem("lo_ok"), sem("mm_ok"), sem("o_ok")
        block = ctx.enter_context(nc.Block())
        static = lambda t: isinstance(t, int)

        def steps(eng, step):
            for t in range(RING):
                step(t, 0, t, 128)
            with eng.Fori(0, FULL_TILES // RING - 1) as k:
                for c in range(RING):
                    step(Count(k, RING, RING + c), Count(k, 1, 1), c, 128)
            step(FULL_TILES, FULL_TILES // RING, 0, TAIL)

        @block.sync
        def _(sp):
            def step(t, turn, c, rows):
                if static(t) and t < RING:
                    return
                sp.wait_ge(lo_ok, val(t - RING + 1))
                sp.dma_start(raw[c][:, :, 0:rows], ct_in[bass.ds(val(t * 128), 128), :, 0:rows]).then_inc(ld[c], 16)
                sp.wait_ge(o_ok, val(t - RING + 1))
                sp.dma_start(h_t[c][0:rows], h2[bass.ds(val(t * 128), rows), :]).then_inc(h_ld[c], 16)

            steps(sp, step)

        @block.scalar
        def _(act):
            def step(t, turn, c, rows):
                act.wait_ge(ld[c], val(16 * (turn + 1)))
                if not static(t) or t >= 2:
                    act.wait_ge(mm_ok, val(t - 1))
                nc.scalar.activation(hi[c % 2][:, :, 0:rows], raw[c][:, :, 0:rows], ACT.Copy).then_inc(hi_ok, 1)

            steps(act, step)

        @block.vector
        def _(dve):
            def finish(t, turn, c, rows):
                dve.wait_ge(mm_ok, val(t + 1))
                dve.wait_ge(h_ld[c], val(16 * (turn + 1)))
                if not static(t) or t >= 2:
                    dve.wait_ge(st[c % 2], val(16 * (2 * turn + c // 2)))
                nc.vector.tensor_tensor(o[c % 2][0:rows], p_o[c % 2][0:rows], h_t[c][0:rows], ALU.add).then_inc(o_ok, 1)

            def step(t, turn, c, rows):
                dve.wait_ge(hi_ok, val(t + 1))
                if not static(t) or t >= 2:
                    dve.wait_ge(mm_ok, val(t - 1))
                nc.vector.tensor_tensor(lo[c % 2][:, :, 0:rows], raw[c][:, :, 0:rows], hi[c % 2][:, :, 0:rows].bitcast(F32),
                                        ALU.subtract).then_inc(lo_ok, 1)
                if not static(t) or t >= 1:
                    finish(t - 1, turn if c else turn - 1, (c - 1) % RING, 128)

            steps(dve, step)
            finish(FULL_TILES, FULL_TILES // RING, 0, TAIL)

        @block.gpsimd
        def _(pool):
            def step(t, turn, c, rows):
                pool.wait_ge(o_ok, val(t + 1))
                pool.dma_start(out[bass.ds(val(t * 128), rows), :], o[c % 2][0:rows]).then_inc(st[c % 2], 16)

            steps(pool, step)
            pool.wait_ge(st[0], 16 * ((TILES + 1) // 2))
            pool.wait_ge(st[1], 16 * (TILES // 2))

        @block.tensor
        def _(pe):
            def step(t, turn, c, rows):
                pe.wait_ge(lo_ok, val(t + 1))
                if not static(t) or t >= 2:
                    pe.wait_ge(o_ok, val(t - 1))
                n = 0
                for a, y in ((hi, y_hi), (hi, y_lo), (lo, y_hi)):
                    for e in range(EB):
                        last = nc.tensor.matmul(p_o[c % 2][0:rows], a[c % 2][:, e, 0:rows], y[:, e, :],
                                                start=n == 0, stop=n == 3 * EB - 1)
                        n += 1
                last.then_inc(mm_ok, 1)

            steps(pe, step)


def program(nc, patches, txt, wt, tok_b, wqk, wv, wo, phi, phi_b, wexp, ebias, rope_cos, rope_sin, identity, out):
    emb = nc.dram_tensor("emb", (BATCH * PATCHES, C), F32, kind="Internal").ap()
    h2 = nc.dram_tensor("h2", (TOKENS, C), F32, kind="Internal").ap()
    ct = nc.dram_tensor("combine_t", (TILES * 128, EB, 128), F32, kind="Internal").ap()

    def parts(ctx, name, shape):
        return [ctx.enter_context(nc.sbuf_tensor(f"{name}_{part}", shape, F32R)) for part in ("hi", "lo")]

    with (nc.sbuf_tensor("ident", [128, 128], F32) as ident, nc.sbuf_tensor("xacc", [128, EB, C], F32) as xacc,
          nc.sbuf_tensor("expert_bias", [128, EB, C], F32) as eb, nc.semaphore("expert_bias_in") as eb_in, ExitStack() as whole):
        with ExitStack() as shared:
            phi_parts = parts(shared, "phi", [128, KC, E])
        w_slots = [whole.enter_context(nc.sbuf_tensor(f"expert_w{i}", [128, EPB, KC, C], F32))[:]
                   for i in range(2 * KC * E // (EPB * KC * C))]
        w_in = [whole.enter_context(nc.semaphore(f"expert_w_in{i}")) for i in range(EXPERT_RING)]
        with ExitStack() as slots:
            bias_rows = slots.enter_context(nc.sbuf_tensor("bias_rows", [64, E], F32R))
            bias_ones = slots.enter_context(nc.sbuf_tensor("bias_ones", [64, 128], F32R))
            with ExitStack() as projections:
                wqk_parts = parts(projections, "wqk", [128, KC, 2 * C])
                wv_parts = parts(projections, "wv", [128, KC, C])
                wo_parts = parts(projections, "wo", [128, KC, C])
                embed(nc, patches, wt, tok_b, emb, [(wqk, *wqk_parts), (wv, *wv_parts), (wo, *wo_parts),
                                                    (phi, *phi_parts)], identity, ident, phi_b, bias_rows, bias_ones)
                attend(nc, emb, txt, rope_cos, rope_sin, ident, wqk_parts, wv_parts, wo_parts, h2)
            dispatch(nc, h2, phi_parts, (bias_rows, bias_ones), ident, xacc, ct, ebias, eb, eb_in, wexp, w_slots, w_in)
        with ExitStack() as outputs:
            y_parts = parts(outputs, "y", [128, EB, C])
            raw = [outputs.enter_context(nc.sbuf_tensor(f"weights{i}", [128, EB, 128], F32)) for i in range(COMBINE_RING)]
            h_t = [outputs.enter_context(nc.sbuf_tensor(f"residual{i}", [128, C], F32)) for i in range(COMBINE_RING)]
            ld = [outputs.enter_context(nc.semaphore(f"weights_in{i}")) for i in range(COMBINE_RING)]
            h_ld = [outputs.enter_context(nc.semaphore(f"residual_in{i}")) for i in range(COMBINE_RING)]
            combine_in = (raw, h_t, ld, h_ld)
            experts(nc, xacc, wexp, w_slots, w_in, eb, eb_in, ident, *y_parts, ct, h2, combine_in)
            combine(nc, ct, h2, *y_parts, combine_in, out)


def kernel(x, txt, L0_tok_W, L0_tok_b, L0_attn_Wq, L0_attn_Wk, L0_attn_Wv, L0_attn_Wo, L0_ffn_phi_w, L0_ffn_phi_b,
           L0_ffn_expert_w, L0_ffn_expert_b):
    import concourse.bacc as bacc
    from concourse.bass_utils import run_bass_kernel_spmd

    a = np.ascontiguousarray
    x, txt = np.asarray(x), np.asarray(txt)
    patches = x.reshape(BATCH, 6, 16, 6, 16, 3).transpose(0, 1, 3, 2, 4, 5).reshape(-1, 128, KP, 128).transpose(0, 3, 2, 1)

    def lead(w, k):
        w = np.asarray(w)
        return w.reshape(w.shape[0], k, 128).transpose(2, 1, 0)

    order = [head_of(g, j) for g in range(GROUPS) for j in range(GH)]
    wo = np.asarray(L0_attn_Wo).reshape(C, HEADS, DH)[:, order, :].reshape(C, C)
    wexp = np.asarray(L0_ffn_expert_w).reshape(EB, EPB, KC, 128, C).transpose(0, 3, 1, 2, 4)
    ebias = np.asarray(L0_ffn_expert_b).reshape(EB, EPB, C).transpose(1, 0, 2)
    inv = 1.0 / 10000.0 ** (np.arange(0, DH, 2, dtype=np.float32) / DH)
    freqs = np.arange(T, dtype=np.float32)[:, None] * inv[None, :]
    cos = np.repeat(np.cos(freqs), 2, axis=1).astype(np.float32)
    sin = np.stack([-np.sin(freqs), np.sin(freqs)], axis=-1).reshape(T, DH).astype(np.float32)
    arrays = {
        "patches": a(patches), "txt": a(txt.reshape(BATCH * WORDS, C)), "wt": a(lead(L0_tok_W, KP)),
        "tok_b": a(np.asarray(L0_tok_b).reshape(1, C)),
        "wqk": a(lead(np.concatenate([np.asarray(L0_attn_Wq), np.asarray(L0_attn_Wk)]), KC)),
        "wv": a(lead(L0_attn_Wv, KC)), "wo": a(lead(wo, KC)), "phi": a(lead(L0_ffn_phi_w, KC)),
        "phi_b": a(np.asarray(L0_ffn_phi_b).reshape(1, E)), "wexp": a(wexp), "ebias": a(ebias),
        "rope_cos": cos, "rope_sin": sin, "identity": np.eye(128, dtype=np.float32),
    }
    nc = bacc.Bacc("TRN2", target_bir_lowering=False, num_devices=1)
    args = {n: nc.dram_tensor(n, v.shape, mybir.dt.from_np(v.dtype), kind="ExternalInput").ap() for n, v in arrays.items()}
    out = nc.dram_tensor("out", (TOKENS, C), F32, kind="ExternalOutput").ap()
    program(nc, out=out, **args)
    r = run_bass_kernel_spmd(nc, [arrays], core_ids=[0])
    return r.results[0]["out"].reshape(BATCH, T, C)
```
